# Optimizing a Trainium2 kernel written in Bass

```python
import numpy as np
import jax
import jax.numpy as jnp

def _softmax(x, axis=-1):
    return jax.nn.softmax(x, axis=axis)

def _gelu(x):
    return jax.nn.gelu(x, approximate=True)

def _silu(x):
    return jax.nn.silu(x)

def _sigmoid(x):
    return jax.nn.sigmoid(x)

def _layernorm(x, axis=-1, eps=1e-05):
    m = jnp.mean(x, axis=axis, keepdims=True)
    v = jnp.var(x, axis=axis, keepdims=True)
    return (x - m) / jnp.sqrt(v + eps)

def _scatter_add(tgt, idx, src, axis=0):
    return tgt.at[idx].add(src)

def _segment_sum(src, seg, n):
    return jax.ops.segment_sum(src, seg, n)
kernel_name = 'mk_seq_postln_d1_jaxref_r8_02b1c3'

def setup_inputs(seed: int=0):
    np.random.seed(seed)
    _w = jnp.asarray

    def _L0_attn_setup():
        import jax, jax.numpy as jnp
        import numpy as np
        B, S, D = (1, 256, 512)
        H = 32
        QL = 192
        KVL = 64
        DN = 128
        DR = 64
        DV = 128
        BASE = 10000.0
        FACTOR = 40.0
        BFAST, BSLOW = (32.0, 1.0)
        OLD_CTX = 4096.0
        MSCALE = 1.0

        def _yarn_inv_freq():
            freqs = 1.0 / BASE ** (jnp.arange(0, DR, 2, dtype=jnp.float32) / DR)
            wavelengths = 2.0 * jnp.pi / freqs
            ramp = jnp.clip((wavelengths / OLD_CTX - BSLOW) / (BFAST - BSLOW), 0.0, 1.0)
            scale = 1.0 - ramp + ramp * FACTOR
            return (freqs / scale, MSCALE)

        def _apply_rope(x, inv_freq, mscale):
            seq = x.shape[-2]
            pos = jnp.arange(seq, dtype=jnp.float32)
            f = jnp.concatenate([pos[:, None] * inv_freq[None, :]] * 2, axis=-1)
            cos = jnp.cos(f) * mscale
            sin = jnp.sin(f) * mscale
            half = DR // 2
            x1, x2 = (x[..., :half], x[..., half:])
            c1, c2 = (cos[:, :half], cos[:, half:])
            s2 = sin[:, half:]
            return jnp.concatenate([x1 * c1 - x2 * s2, x1 * s2 + x2 * c2], axis=-1)
        key = jax.random.key(seed)
        ks = jax.random.split(key, 10)

        def glorot(k, shape):
            lim = np.sqrt(6.0 / (shape[0] + shape[1])).astype(np.float32)
            return jax.random.uniform(k, shape, jnp.float32, -lim, lim)
        return {'hidden_states': jax.random.normal(ks[0], (B, S, D), jnp.float32), 'w_q_down': glorot(ks[1], (D, QL)), 'w_q_up_nope': glorot(ks[2], (QL, H * DN)), 'w_q_up_rope': glorot(ks[3], (QL, H * DR)), 'w_kv_down': glorot(ks[4], (D, KVL)), 'w_k_rope': glorot(ks[5], (D, DR)), 'w_uk': glorot(ks[6], (H * DN, KVL)), 'w_uv': glorot(ks[7], (H * DV, KVL)), 'w_out': glorot(ks[8], (H * DV, D))}
    _L0_attn_in = _L0_attn_setup()

    def _L0_ffn_setup():
        import jax, jax.numpy as jnp
        import numpy as np
        R = 16
        NUM_EXPERTS = 8
        TOP_K = 2
        LORA_ALPHA = 32
        SCALING = LORA_ALPHA / R
        key = jax.random.key(seed)
        ks = jax.random.split(key, 6)
        d_in, d_out = (512, 512)
        x = jax.random.normal(ks[0], (4, 256, d_in), dtype=jnp.float32)
        W_base = jax.random.normal(ks[1], (d_out, d_in), dtype=jnp.float32) * 0.02
        b_base = jax.random.normal(ks[2], (d_out,), dtype=jnp.float32) * 0.02
        W_router = jax.random.normal(ks[3], (NUM_EXPERTS, d_in), dtype=jnp.float32) * 0.01
        A = jax.random.normal(ks[4], (NUM_EXPERTS, R, d_in), dtype=jnp.float32) * 0.02
        B = jax.random.normal(ks[5], (NUM_EXPERTS, d_out, R), dtype=jnp.float32) * 0.02
        return {'x': x, 'W_base': W_base, 'b_base': b_base, 'W_router': W_router, 'A': A, 'B': B}
    _L0_ffn_in = _L0_ffn_setup()
    _d = {'L0_attn_hidden_states': _L0_attn_in['hidden_states'], 'L0_attn_w_q_down': _L0_attn_in['w_q_down'], 'L0_attn_w_q_up_nope': _L0_attn_in['w_q_up_nope'], 'L0_attn_w_q_up_rope': _L0_attn_in['w_q_up_rope'], 'L0_attn_w_kv_down': _L0_attn_in['w_kv_down'], 'L0_attn_w_k_rope': _L0_attn_in['w_k_rope'], 'L0_attn_w_uk': _L0_attn_in['w_uk'], 'L0_attn_w_uv': _L0_attn_in['w_uv'], 'L0_attn_w_out': _L0_attn_in['w_out'], 'L0_ffn_W_base': _L0_ffn_in['W_base'], 'L0_ffn_b_base': _L0_ffn_in['b_base'], 'L0_ffn_W_router': _L0_ffn_in['W_router'], 'L0_ffn_A': _L0_ffn_in['A'], 'L0_ffn_B': _L0_ffn_in['B']}
    _x0 = _d['L0_attn_hidden_states']
    _d['L0_attn_hidden_states'] = jax.random.normal(jax.random.fold_in(jax.random.key(seed), 1), (1, 1024, 512), dtype=_x0.dtype)
    del _x0
    return _d

def reference(L0_attn_hidden_states, L0_attn_w_q_down, L0_attn_w_q_up_nope, L0_attn_w_q_up_rope, L0_attn_w_kv_down, L0_attn_w_k_rope, L0_attn_w_uk, L0_attn_w_uv, L0_attn_w_out, L0_ffn_W_base, L0_ffn_b_base, L0_ffn_W_router, L0_ffn_A, L0_ffn_B):

    def _L0_attn_ref(hidden_states, w_q_down, w_q_up_nope, w_q_up_rope, w_kv_down, w_k_rope, w_uk, w_uv, w_out):
        import jax, jax.numpy as jnp
        import numpy as np
        B, S, D = (1, 256, 512)
        H = 32
        QL = 192
        KVL = 64
        DN = 128
        DR = 64
        DV = 128
        BASE = 10000.0
        FACTOR = 40.0
        BFAST, BSLOW = (32.0, 1.0)
        OLD_CTX = 4096.0
        MSCALE = 1.0

        def _yarn_inv_freq():
            freqs = 1.0 / BASE ** (jnp.arange(0, DR, 2, dtype=jnp.float32) / DR)
            wavelengths = 2.0 * jnp.pi / freqs
            ramp = jnp.clip((wavelengths / OLD_CTX - BSLOW) / (BFAST - BSLOW), 0.0, 1.0)
            scale = 1.0 - ramp + ramp * FACTOR
            return (freqs / scale, MSCALE)

        def _apply_rope(x, inv_freq, mscale):
            seq = x.shape[-2]
            pos = jnp.arange(seq, dtype=jnp.float32)
            f = jnp.concatenate([pos[:, None] * inv_freq[None, :]] * 2, axis=-1)
            cos = jnp.cos(f) * mscale
            sin = jnp.sin(f) * mscale
            half = DR // 2
            x1, x2 = (x[..., :half], x[..., half:])
            c1, c2 = (cos[:, :half], cos[:, half:])
            s2 = sin[:, half:]
            return jnp.concatenate([x1 * c1 - x2 * s2, x1 * s2 + x2 * c2], axis=-1)
        b, s, _ = hidden_states.shape
        c_q = hidden_states @ w_q_down
        q_nope = (c_q @ w_q_up_nope).reshape(b, s, H, DN).transpose(0, 2, 1, 3)
        q_rope = (c_q @ w_q_up_rope).reshape(b, s, H, DR).transpose(0, 2, 1, 3)
        c_kv = hidden_states @ w_kv_down
        k_rope = (hidden_states @ w_k_rope)[:, None]
        inv_freq, mscale = _yarn_inv_freq()
        q_rope = _apply_rope(q_rope, inv_freq, mscale)
        k_rope = _apply_rope(k_rope, inv_freq, mscale)
        wuk = w_uk.reshape(H, DN, KVL)
        q_lat = jnp.einsum('bhsd,hdr->bhsr', q_nope, wuk)
        scores = jnp.einsum('bhsr,btr->bhst', q_lat, c_kv) + jnp.einsum('bhsd,btd->bhst', q_rope, k_rope[:, 0])
        scores = scores / jnp.sqrt(jnp.float32(DN + DR))
        causal = jnp.tril(jnp.ones((s, s), dtype=bool))
        scores = jnp.where(causal, scores, jnp.finfo(scores.dtype).min)
        probs = jax.nn.softmax(scores, axis=-1)
        out_lat = jnp.einsum('bhst,btr->bhsr', probs, c_kv)
        wuv = w_uv.reshape(H, DV, KVL)
        out = jnp.einsum('bhsr,hdr->bhsd', out_lat, wuv)
        out = out.transpose(0, 2, 1, 3).reshape(b, s, H * DV)
        return out @ w_out

    def _L0_ffn_ref(x, W_base, b_base, W_router, A, B):
        import jax, jax.numpy as jnp
        import numpy as np
        R = 16
        NUM_EXPERTS = 8
        TOP_K = 2
        LORA_ALPHA = 32
        SCALING = LORA_ALPHA / R
        orig_shape = x.shape
        d_in = x.shape[-1]
        x_flat = x.reshape(-1, d_in)
        logits = x_flat @ W_router.T
        probs = jax.nn.softmax(logits, axis=-1)
        topk_probs, topk_idx = jax.lax.top_k(probs, TOP_K)
        topk_probs = topk_probs / jnp.sum(topk_probs, axis=-1, keepdims=True)
        onehot = jax.nn.one_hot(topk_idx, NUM_EXPERTS, dtype=x.dtype)
        combine = jnp.einsum('nk,nke->ne', topk_probs, onehot)
        h = jnp.einsum('nd,erd->ner', x_flat, A)
        hw = h * combine[:, :, None]
        expert_out = jnp.einsum('ner,eor->no', hw, B) * SCALING
        base_out = x_flat @ W_base.T + b_base
        out = base_out + expert_out
        return out.reshape(*orig_shape[:-1], W_base.shape[0])
    x = L0_attn_hidden_states
    x = _layernorm(x + _L0_attn_ref(x, L0_attn_w_q_down, L0_attn_w_q_up_nope, L0_attn_w_q_up_rope, L0_attn_w_kv_down, L0_attn_w_k_rope, L0_attn_w_uk, L0_attn_w_uv, L0_attn_w_out), axis=-1)
    x = _layernorm(x + _L0_ffn_ref(x, L0_ffn_W_base, L0_ffn_b_base, L0_ffn_W_router, L0_ffn_A, L0_ffn_B), axis=-1)
    return x

_drawn_inputs = setup_inputs


def setup_inputs(seed=0):
    import zlib

    import numpy as np

    out = dict(_drawn_inputs(seed))
    spreads = {}
    factors = {'L0_attn_w_q_down': 5.36,
     'L0_attn_w_q_up_nope': 8.0,
     'L0_attn_w_q_up_rope': 5.65,
     'L0_attn_w_k_rope': 5.573,
     'L0_attn_w_uk': 8.0,
     'L0_ffn_b_base': 3.244}
    for name, (base, spread) in spreads.items():
        noise = np.random.default_rng([zlib.crc32(name.encode()), seed]).standard_normal(out[name].shape)
        drawn = base * np.exp(spread * noise) if base else spread * noise
        out[name] = jnp.asarray(drawn.astype(out[name].dtype))
    for name, factor in factors.items():
        out[name] = (out[name] * factor).astype(out[name].dtype)
    return out
```

```python
from contextlib import ExitStack

import concourse.bass as bass
from concourse import mybir

F32 = mybir.dt.float32
F32R = mybir.dt.float32r
BF16 = mybir.dt.bfloat16
ALU = mybir.AluOpType
ACT = mybir.ActivationFunctionType
AX_X = mybir.AxisListType.X

P = 128
S = 1024
D = 512
H = 32
QL = 192
R = 64
DN = 128
PAIRS = H // 2
T = S // P
KD = D // P
BANK = 512
NE, RANK = 8, 16
LORA_SCALE = 32 / RANK
EPS = 1e-5
SCALE = float(1.0 / (DN + R) ** 0.5)

ROW_W = [S - P * j for j in range(T)]
ROW_AT = [sum(ROW_W[:j]) for j in range(T)]
HEAD_COLS = sum(ROW_W)
CHUNKS = [(0,), (1, 2), (3, 4), (5, 6, 7)]
CHUNK_OF = [c for j in range(T) for c in range(len(CHUNKS)) if j in CHUNKS[c]]

Z_AT, A_AT, B_AT, ST_W = 0, 128, 256, 384
UNF = 16

PRE_JOBS = ["cq1_0", "cq1_1", "cq2_0", "cq2_1"] + [f"k{n}_{c}" for c in range(2) for n in "zab"] \
    + ["v_0", "v_1", "m"] + [f"f{n}_{c}" for c in range(2) for n in "zab"]


def step_jobs(g):
    s, f, p, o = g < PAIRS, g + 1 < PAIRS, 1 <= g <= PAIRS, g >= 2
    jobs = []
    if s:
        jobs += ["ta_0", "ta_1"]
    if f:
        jobs += ["m"]
    if o:
        jobs += [f"o_{i}" for i in range(4)]
    if s:
        jobs += ["tb_0", "tb_1"]
    if f:
        jobs += [f"f{n}_{c}" for c in range(2) for n in "zab"]
    if o:
        jobs += [f"o_{i}" for i in range(4, 8)]
    if p:
        jobs += ["la_0", "la_1", "n", "lb_0", "lb_1"]
    return jobs


STEPS = PAIRS + 2
BASE = [len(PRE_JOBS)]
for _g in range(STEPS):
    BASE.append(BASE[-1] + len(step_jobs(_g)))
STEADY = 2
JOBS_PER_STEP = BASE[STEADY + 1] - BASE[STEADY]
assert JOBS_PER_STEP % 2 == 0


LAST_READ = [2 * ((BASE[-1] + 1) // 2), 2 * (BASE[-1] // 2)]


class Job:

    def __init__(self, g, name, back=0):
        if g is None:
            at, extra = PRE_JOBS.index(name), 0
        elif isinstance(g, int):
            at, extra = BASE[g - back] + step_jobs(g - back).index(name), 0
        else:
            at, extra = BASE[STEADY] + step_jobs(STEADY).index(name), g - (STEADY + back)
        self.bank = at % 2
        self.done = extra * JOBS_PER_STEP + (at + 1)
        self.earlier = at // 2
        self.free = extra * JOBS_PER_STEP + 2 * (at // 2)
        self.read = extra * JOBS_PER_STEP + 2 * (at // 2 + 1)


def build(nc, xT, xres, wq_down, wk, qw, ow, tables, ident, ident16, mask16, rank_tab, ffn_w, bias, out):
    with ExitStack() as ctx:
        def sb(name, shape, dt=F32):
            return ctx.enter_context(nc.sbuf_tensor(name, shape, dt))

        def ps(name, shape, dt=F32):
            return ctx.enter_context(nc.psum_tensor(name, shape, dt))

        def sem(name):
            return ctx.enter_context(nc.semaphore(name))

        ring = sb("ring", [P, 4, HEAD_COLS])
        key_hi = sb("key_hi", [P, 2, S], F32R)
        key_lo = sb("key_lo", [P, 2, S], F32R)
        q_hi = sb("q_hi", [P, 2, S], F32R)
        q_lo = sb("q_lo", [P, 2, S], F32R)
        turned = sb("turned", [P, BANK])
        fused = sb("fused", [P, 2, BANK])
        cos_sin = sb("cos_sin", [P, 2, S])
        c1_hi = sb("c1_hi", [P, S], F32R)
        c1_lo = sb("c1_lo", [P, S], F32R)
        c2_hh = sb("c2_hh", [P, S], F32R)
        c2_lo = sb("c2_lo", [R, S], F32R)
        top = sb("top", [P, 2, S])
        psum_p = sb("psum_p", [P, 2, S])
        maxes = sb("maxes", [P, 2, S])
        att = sb("att", [P, S])
        att_hi = sb("att_hi", [P, S], F32R)
        att_lo = sb("att_lo", [P, S], F32R)
        n_hi = sb("n_hi", [P, D], F32R)
        n_lo = sb("n_lo", [P, D], F32R)
        qw_sb = sb("qw_sb", [P, 2 * 256 + 2 * R + 512])
        ow_sb = sb("ow_sb", [P, 2 * R + 2 * D])
        st1_hi = sb("st1_hi", [P, ST_W], F32R)
        st1_lo = sb("st1_lo", [P, ST_W], F32R)
        st2 = sb("st2", [P, ST_W], F32R)
        y = sb("y", [P, T, D])
        values = sb("values", [P, T, R])
        id32 = sb("id32", [P, P])
        id16 = sb("id16", [P, P], BF16)
        causal16 = sb("causal16", [P, P], BF16)
        max_col = sb("max_col", [P, 2, T])
        sum_col = sb("sum_col", [P, 2, T])
        inv_col = sb("inv_col", [P, 2, T])

        row_ps = ps("row_ps", [P, 2, 2 * BANK])
        att_ps = ps("att_ps", [P, 2, BANK])
        job_ps = ps("job_ps", [P, 2, BANK])

        max_dram = nc.dram_tensor("max_rows", (2, S), F32, kind="Internal").ap()
        inv_dram = nc.dram_tensor("inv_rows", (2, S), F32, kind="Internal").ap()

        def row(slot, j):
            return ring[:, slot, ROW_AT[j]:ROW_AT[j] + ROW_W[j]]

        flat = ring[:, :, :].rearrange("p a n -> p (a n)")
        at = [0]

        def carve(n):
            at[0] += n
            return flat[:, at[0] - n:at[0]]

        xT_sb = carve(KD * S).rearrange("p (k s) -> p k s", k=KD)
        wqd_sb = carve(KD * 256).rearrange("p (k n) -> p k n", k=KD)
        wk_sb = carve(KD * 384).rearrange("p (k n) -> p k n", k=KD)
        assert at[0] <= 2 * HEAD_COLS
        at[0] = 0
        HW = NE * RANK + NE
        base_w = carve(KD * D).rearrange("p (k n) -> p k n", k=KD)
        hr_w = carve(KD * HW).rearrange("p (k n) -> p k n", k=KD)
        up_w = carve(D)
        bias_sb = carve(D)
        rank_sb = carve(T * NE).rearrange("p (i e) -> p i e", e=NE)
        ffn_loaded_cols = at[0]
        x1T = carve(KD * S).rearrange("p (k s) -> p k s", k=KD)
        assert at[0] <= 2 * HEAD_COLS
        at[0] = 2 * HEAD_COLS
        hr = carve(T * HW).rearrange("p (i n) -> p i n", i=T)
        hT = carve(S)
        small = [carve(T * NE).rearrange("p (i e) -> p i e", e=NE) for _ in range(8)]
        thin = [carve(T) for _ in range(10)]
        stats = carve(T * 6).rearrange("p (i n) -> p i n", i=T)
        moments = carve(T * 2).rearrange("p (i n) -> p i n", i=T)
        eps_sb = carve(1)
        hw = carve(T * P).rearrange("p (i n) -> p i n", i=T)
        res = carve(T * D).rearrange("p (i n) -> p i n", i=T)
        assert at[0] <= 4 * HEAD_COLS

        qnT = [qw_sb[:, h * 256:(h + 1) * 256] for h in range(2)]
        wuk = [qw_sb[:, 512 + h * R:512 + (h + 1) * R] for h in range(2)]
        wr1 = qw_sb[:, 640:896]
        wr2 = qw_sb[:, 896:1152]
        wuv = [ow_sb[:, h * R:(h + 1) * R] for h in range(2)]
        wout = [ow_sb[:, 128 + h * D:128 + (h + 1) * D] for h in range(2)]

        def rot_cols(t):
            return t.rearrange("p (a b) -> p a b", b=192)[:, :, 0:128]

        def lat_cols(t):
            return t.rearrange("p (a b) -> p a b", b=192)[:, :, 128:192]

        ld_cq = sem("ld_cq")
        ld_k = sem("ld_k")
        ld_tab = sem("ld_tab")
        ld_id = sem("ld_id")
        ld_y = sem("ld_y")
        ld_qw = sem("ld_qw")
        ld_ow = sem("ld_ow")
        ld_ffn = sem("ld_ffn")
        max_written = sem("max_written")
        max_loaded = [sem("max_loaded_a"), sem("max_loaded_b")]
        inv_written = sem("inv_written")
        inv_loaded = sem("inv_loaded")
        job_done = sem("job_done")
        job_read = [sem("job_read_0"), sem("job_read_1")]
        row_done = sem("row_done")
        row_copied = sem("row_copied")
        row_maxed = sem("row_maxed")
        centred = sem("centred")
        exped = sem("exped")
        summed = sem("summed")
        inv_ready = sem("inv_ready")
        att_done = sem("att_done")
        att_scaled = sem("att_scaled")
        att_hi_set = sem("att_hi_set")
        att_lo_set = sem("att_lo_set")
        n_hi_set = sem("n_hi_set")
        c_hi_set = sem("c_hi_set")
        rot_set = sem("rot_set")
        fused_set = sem("fused_set")
        qk_hi_set = sem("qk_hi_set")
        qk_lo_set = sem("qk_lo_set")
        st_rot_hi = sem("st_rot_hi")
        st_rot_lo = sem("st_rot_lo")
        st_lat_hi = sem("st_lat_hi")
        st_lat_lo = sem("st_lat_lo")
        y_set = sem("y_set")
        mean_linked = sem("mean_linked")
        spread_ready = sem("spread_ready")
        x1_set = sem("x1_set")
        x1_turned = sem("x1_turned")
        x1T_set = sem("x1T_set")
        hr_done = sem("hr_done")
        hr_set = sem("hr_set")
        logits_centred = sem("logits_centred")
        logits_exped = sem("logits_exped")
        hw_set = sem("hw_set")
        hw_turned = sem("hw_turned")
        hT_set = sem("hT_set")
        ff_done = sem("ff_done")
        x1b_set = sem("x1b_set")
        var_ready = sem("var_ready")
        sd_ready = sem("sd_ready")
        res_set = sem("res_set")
        out_written = sem("out_written")

        def run_steps(eng, step):
            step(0, 0)
            step(1, 1)
            with eng.Fori(STEADY, PAIRS - 2, 2) as g:
                step(g, 0)
                step(g + 1, 1)
            for g in range(PAIRS - 2, STEPS):
                step(g, g % 2)

        def ffn_banks(rows, jobs):
            return [att_ps[:, 0, :], att_ps[:, 1, :], *jobs, *rows]

        def parts(g):
            if not isinstance(g, int):
                return True, True, True, True
            return g < PAIRS, g + 1 < PAIRS, 1 <= g <= PAIRS, g >= 2

        block = ctx.enter_context(nc.Block())

        @block.sync
        def _(sp):
            sp.dma_start(wqd_sb, wq_down).then_inc(ld_cq, 16)
            for k in range(KD):
                sp.dma_start(xT_sb[:, k, :], xT[:, k, :]).then_inc(ld_cq, 16)
            sp.dma_start(wk_sb, wk).then_inc(ld_k, 16)
            sp.dma_start(cos_sin[:, :, :], tables).then_inc(ld_tab, 16)
            sp.dma_start(qw_sb[:, :], qw[0, :, :]).then_inc(ld_qw, 16)
            sp.dma_start(id32[:, :], ident).then_inc(ld_id, 16)
            sp.dma_start(id16[:, :], ident16).then_inc(ld_id, 16)
            sp.dma_start(causal16[:, :], mask16).then_inc(ld_id, 16)
            sp.dma_start(ow_sb[:, :], ow[0, :, :]).then_inc(ld_ow, 16)
            sp.dma_start(y[:, :, :], xres.rearrange("(i p) d -> p i d", p=P)).then_inc(ld_y, 16)

            def values_of(*targets):
                return [t if isinstance(t, int) else sp.to_reg(t) for t in targets]

            def maxima(g, h):
                turned_jobs = [Job(g, f"t{'ab'[h]}_{c}") for c in range(2)]
                read0, read1, written, used = values_of(turned_jobs[0].read, turned_jobs[1].read,
                                                        (2 * g + h + 1) * UNF, (2 * g + h - 1) * T)
                sp.wait_ge(job_read[turned_jobs[0].bank], read0)
                sp.wait_ge(job_read[turned_jobs[1].bank], read1)
                sp.dma_start(max_dram[h, :].rearrange("(p i) -> p i", i=T), max_col[:, h, :]).then_inc(max_written, 16)
                sp.wait_ge(max_written, written)
                if not isinstance(g, int) or g > 0:
                    sp.wait_ge(centred, used)
                sp.dma_start(maxes[:, h, :], max_dram[h:h + 1, :].partition_broadcast(P).rearrange("p a s -> p (a s)")
                             ).then_inc(max_loaded[h], 16)

            def step(g, par):
                scores, queries, vals, _ = parts(g)
                if queries:
                    sp.wait_ge(st_lat_lo, g + 1)
                    sp.wait_ge(st_rot_hi, 2 * g + 2)
                    sp.wait_ge(st_rot_lo, 2 * g + 2)
                    src = qw[g + 1, :, :] if isinstance(g, int) else qw[bass.ds(g + 1, 1), :, :].rearrange("a p n -> p (a n)")
                    sp.dma_start(qw_sb[:, :], src).then_inc(ld_qw, 16)
                if scores:
                    maxima(g, 0)
                    maxima(g, 1)
                if vals:
                    ready0, ready1, written, split, n_made = values_of(2 * g - 1, 2 * g, g * (2 * UNF), g - 1, g)
                    sp.wait_ge(inv_ready, ready0)
                    sp.dma_start(inv_dram[0, :].rearrange("(p i) -> p i", i=T), inv_col[:, 0, :]).then_inc(inv_written, 16)
                    sp.wait_ge(inv_ready, ready1)
                    sp.dma_start(inv_dram[1, :].rearrange("(p i) -> p i", i=T), inv_col[:, 1, :]).then_inc(inv_written, 16)
                    if not isinstance(g, int) or g > 1:
                        sp.wait_ge(att_lo_set, split)
                    sp.wait_ge(inv_written, written)
                    for h in range(2):
                        sp.dma_start(att[R * h:R * h + R, :],
                                     inv_dram[h:h + 1, :].partition_broadcast(R).rearrange("p a s -> p (a s)")
                                     ).then_inc(inv_loaded, 16)
                    if scores:
                        sp.wait_ge(n_hi_set, g)
                        src = ow[g, :, :] if isinstance(g, int) else ow[bass.ds(g, 1), :, :].rearrange("a p n -> p (a n)")
                        sp.dma_start(ow_sb[:, :], src).then_inc(ld_ow, 16)
                if isinstance(g, int) and g == PAIRS:
                    sp.wait_ge(att_done, PAIRS - 1)
                    sp.wait_ge(summed, 2 * T * (PAIRS - 1))
                    n = KD * D + KD * HW + D
                    sp.dma_start(flat[:, 0:n], ffn_w).then_inc(ld_ffn, 16)
                    sp.dma_start(bias_sb, bias.partition_broadcast(P).rearrange("p a s -> p (a s)")).then_inc(ld_ffn, 16)
                    sp.dma_start(flat[:, n + D:n + D + T * NE], rank_tab).then_inc(ld_ffn, 16)

            run_steps(sp, step)
            for i in range(T):
                sp.wait_ge(res_set, i + 1)
                sp.dma_start(out[i * P:(i + 1) * P, :], res[:, i, :]).then_inc(out_written, 16)
            sp.wait_ge(out_written, 16 * T)

        @block.tensor
        def _(pe):
            def open_job(g, name):
                job = Job(g, name)
                if g is not None or job.earlier > 0:
                    pe.wait_ge(job_read[job.bank], job.free)
                return job_ps[:, job.bank, :]

            def queries(g, step_g):
                pe.wait_ge(st_rot_hi, 2 * g + 2)
                pe.wait_ge(st_rot_lo, 2 * g + 2)
                pe.wait_ge(st_lat_hi, 2 * g + 2)
                m = Job(step_g, "m")
                pe.wait_ge(st_lat_lo, g + 1)
                pe.wait_ge(job_read[m.bank], m.read)
                for c in range(2):
                    s0, s1 = c * BANK, (c + 1) * BANK
                    for name, col in (("z", Z_AT), ("a", A_AT), ("b", B_AT)):
                        o = open_job(step_g, f"f{name}_{c}")
                        w = slice(col, col + P)
                        passes = [(st1_hi[:, w], c1_hi[:, s0:s1]), (st1_hi[:, w], c1_lo[:, s0:s1]),
                                  (st1_lo[:, w], c1_hi[:, s0:s1]), (st2[:, w], c2_hh[:, s0:s1]),
                                  (st2[0:R, w], c2_lo[:, s0:s1])]
                        for n, (a, b) in enumerate(passes):
                            mm = pe.matmul(o, a, b, start=(n == 0), stop=(n == len(passes) - 1))
                        mm.then_inc(job_done, 1)

            def fuse_q(g, step_g):
                pe.wait_ge(ld_qw, UNF * (g + 1))
                o = open_job(step_g, "m")
                for n in range(4):
                    half, h = n // 2, n % 2
                    mm = pe.matmul(o[:, n * R:(n + 1) * R], qnT[h][:, half * P:(half + 1) * P], wuk[h],
                                   start=(n == 0), stop=(n == 3), skip_group_check=True)
                mm.then_inc(job_done, 1)

            def score_row(g, h, j):
                n = (2 * g + h) * T + j
                if not (isinstance(g, int) and g == 0 and h == 0 and j < 2):
                    pe.wait_ge(row_copied, n - 1)
                chunks = 2 if ROW_W[j] > BANK else 1
                w = ROW_W[j] // chunks
                for c in range(chunks):
                    o = row_ps[:, j % 2, c * BANK:c * BANK + w]
                    q0 = P * j + c * w
                    kk = slice(P * j, P * j + P)
                    pe.matmul(o, key_hi[:, h, kk], q_hi[:, h, q0:q0 + w], start=True, stop=False)
                    pe.matmul(o, key_hi[:, h, kk], q_lo[:, h, q0:q0 + w], start=False, stop=False)
                    if c == 0:
                        pe.matmul(o[:, 0:P], id16[:, :], causal16[:, :], start=False, stop=False)
                    mm = pe.matmul(o, key_lo[:, h, kk], q_hi[:, h, q0:q0 + w], start=False, stop=True)
                mm.then_inc(row_done, 1)

            def turn(g, kind, h, src):
                v = src.rearrange("p (q i) -> p i q", i=T)
                for c in range(2):
                    o = open_job(g, f"{kind}{'ab'[h]}_{c}")
                    for i in range(4):
                        mm = pe.transpose(o[:, P * i:P * i + P], v[:, 4 * c + i, :], id32[:, :])
                    mm.then_inc(job_done, 1)

            def step(g, par):
                scores, queries_, vals, output = parts(g)
                if scores:
                    pe.wait_ge(qk_hi_set, 4 * (g + 2))
                    pe.wait_ge(qk_lo_set, 4 * (g + 2))
                    for j in range(T):
                        score_row(g, 0, j)
                    for j in range(4):
                        score_row(g, 1, j)
                    pe.wait_ge(row_maxed, (2 * g + 1) * T)
                    turn(g, "t", 0, top[:, 0, :])
                    for j in range(4, T):
                        score_row(g, 1, j)
                if queries_:
                    fuse_q(g + 1, g)

                def outputs(lo, hi):
                    for i in range(lo, hi):
                        o = open_job(g, f"o_{i}")
                        a, b = att_hi[:, i * P:(i + 1) * P], att_lo[:, i * P:(i + 1) * P]
                        pe.matmul(o, a, n_hi[:, :], start=True, stop=False)
                        pe.matmul(o, a, n_lo[:, :], start=False, stop=False)
                        pe.matmul(o, b, n_hi[:, :], start=False, stop=True).then_inc(job_done, 1)

                if output:
                    pe.wait_ge(att_hi_set, g - 1)
                    pe.wait_ge(att_lo_set, g - 1)
                    n_job = Job(g, "n", back=1)
                    pe.wait_ge(n_hi_set, g - 1)
                    pe.wait_ge(job_read[n_job.bank], n_job.read)
                    outputs(0, 4)
                if scores:
                    pe.wait_ge(row_maxed, (2 * g + 2) * T)
                    turn(g, "t", 1, top[:, 1, :])
                if queries_:
                    queries(g + 1, g)
                if output:
                    outputs(4, 8)
                if vals:
                    pe.wait_ge(summed, (2 * g - 1) * T)
                    turn(g, "l", 0, psum_p[:, 0, :])
                    if output:
                        pe.wait_ge(att_scaled, g - 1)
                    slot = 2 * (1 - par)
                    for j in range(T):
                        pe.wait_ge(exped, (2 * g - 1) * len(CHUNKS) + CHUNK_OF[j] + 1)
                        for c in range(2):
                            s0, s1 = max(c * BANK, P * j), (c + 1) * BANK
                            if s0 >= s1:
                                continue
                            for h in range(2):
                                mm = pe.matmul(att_ps[R * h:R * h + R, c, s0 - c * BANK:], values[:, j, :],
                                               row(slot + h, j)[:, s0 - P * j:s1 - P * j],
                                               start=(j == 0), stop=(j == 4 * c + 3))
                    mm.then_inc(att_done, 1)
                    pe.wait_ge(ld_ow, UNF * g)
                    o = open_job(g, "n")
                    for h in range(2):
                        mm = pe.matmul(o[R * h:R * h + R, :], wuv[h], wout[h], start=True, stop=True)
                    mm.then_inc(job_done, 1)
                    pe.wait_ge(summed, 2 * g * T)
                    turn(g, "l", 1, psum_p[:, 1, :])

            pe.wait_ge(ld_cq, 5 * UNF)
            for part in range(2):
                for c in range(2):
                    o = open_job(None, f"cq{part + 1}_{c}")
                    for k in range(KD):
                        mm = pe.matmul(o, wqd_sb[:, k, part * P:(part + 1) * P], xT_sb[:, k, c * BANK:(c + 1) * BANK],
                                       start=(k == 0), stop=(k == KD - 1))
                    mm.then_inc(job_done, 1)
            pe.wait_ge(ld_k, UNF)
            for c in range(2):
                for n, name in enumerate("zab"):
                    o = open_job(None, f"k{name}_{c}")
                    for k in range(KD):
                        mm = pe.matmul(o, wk_sb[:, k, n * P:(n + 1) * P], xT_sb[:, k, c * BANK:(c + 1) * BANK],
                                       start=(k == 0), stop=(k == KD - 1))
                    mm.then_inc(job_done, 1)
            for c in range(2):
                o = open_job(None, f"v_{c}")
                for i in range(4):
                    t = 4 * c + i
                    for k in range(KD):
                        mm = pe.matmul(o[:, i * R:(i + 1) * R], xT_sb[:, k, t * P:(t + 1) * P], wk_sb[:, k, P:P + R],
                                       start=(k == 0), stop=(k == KD - 1))
                mm.then_inc(job_done, 1)
            fuse_q(0, None)
            pe.wait_ge(c_hi_set, 4)
            for c in range(2):
                j = Job(None, f"cq2_{c}")
                pe.wait_ge(job_read[j.bank], j.read)
            queries(0, None)
            pe.wait_ge(ld_id, 3 * UNF)
            for c in range(2):
                j = Job(None, f"v_{c}")
                pe.wait_ge(job_read[j.bank], j.read)
            run_steps(pe, step)

            rows = [row_ps[:, n // 2, (n % 2) * BANK:(n % 2 + 1) * BANK] for n in range(4)]
            jobs = [job_ps[:, n, :] for n in range(2)]
            for n in range(2):
                pe.wait_ge(job_read[n], LAST_READ[n])
            for i in range(T):
                pe.wait_ge(x1_set, i + 1)
                if i >= 2:
                    pe.wait_ge(x1T_set, i - 1)
                for k in range(KD):
                    mm = pe.transpose(jobs[i % 2][:, k * P:(k + 1) * P], y[:, i, k * P:(k + 1) * P], id32[:, :])
                mm.then_inc(x1_turned, 1)
            pe.wait_ge(ld_ffn, 3 * UNF)
            for i in range(T):
                pe.wait_ge(x1T_set, i + 1)
                if i >= 4:
                    pe.wait_ge(hr_set, i - 3)
                for k in range(KD):
                    mm = pe.matmul(rows[i % 4][:, 0:HW], x1T[:, k, i * P:(i + 1) * P], hr_w[:, k, :],
                                   start=(k == 0), stop=(k == KD - 1))
                mm.then_inc(hr_done, 1)

            ff_banks = ffn_banks(rows, jobs)

            def base(i):
                for k in range(KD):
                    pe.matmul(ff_banks[i], x1T[:, k, i * P:(i + 1) * P], base_w[:, k, :], start=(k == 0), stop=False)

            def lora_up(i):
                pe.matmul(ff_banks[i], hT[:, i * P:(i + 1) * P], up_w, start=False, stop=True).then_inc(ff_done, 1)

            for i in range(4):
                base(i)
            pe.wait_ge(hr_set, T)
            for i in range(4, 6):
                base(i)
            pe.wait_ge(hw_set, 1)
            for c in range(2):
                for i in range(4):
                    mm = pe.transpose(rows[2 + c][:, i * P:(i + 1) * P], hw[:, 4 * c + i, :], id32[:, :])
                mm.then_inc(hw_turned, 1)
            pe.wait_ge(hT_set, 2)
            for i in range(6):
                lora_up(i)
            for i in range(6, T):
                base(i)
                lora_up(i)

        @block.scalar
        def _(act):
            def job(g, name):
                j = Job(g, name)
                act.wait_ge(job_done, j.done)
                return job_ps[:, j.bank, :], job_read[j.bank]

            def rotary_weights(g):
                act.wait_ge(ld_qw, UNF * (g + 1))
                for st, raw in ((st1_hi, wr1), (st2, wr2)):
                    act.activation(rot_cols(st[:, :]), raw.rearrange("p (a b) -> p a b", a=2), ACT.Copy
                                   ).then_inc(st_rot_hi, 1)

            def latent_weights(step_g):
                o, _ = job(step_g, "m")
                for n, st in enumerate((st1_hi, st2)):
                    act.activation(lat_cols(st[:, :]), o[:, n * P:(n + 1) * P].rearrange("p (a b) -> p a b", a=2),
                                   ACT.Copy).then_inc(st_lat_hi, 1)

            def queries(n, step_g, kind, hi):
                for c in range(2):
                    for h in range(2):
                        o, read = job(step_g, f"{kind}{'ab'[h]}_{c}")
                        lat = slice(R * h, R * h + R)
                        if c > 0 or not isinstance(n, int) or n > 0:
                            act.wait_ge(qk_lo_set, 4 * n + 2 * c + h - 1)
                        act.wait_ge(rot_set, 4 * n + 2 * c + h + 1)
                        act.activation(fused[lat, h, :], o[lat, :], ACT.Copy).then_inc(read, 2)
                    for h in range(2):
                        act.wait_ge(fused_set, 4 * n + 2 * c + h + 1)
                        j = Job(step_g, f"{kind}{'ab'[h]}_{c}")
                        act.wait_ge(job_read[j.bank], j.read)
                        act.activation(hi[:, h, c * BANK:(c + 1) * BANK], fused[:, h, :], ACT.Copy
                                       ).then_inc(qk_hi_set, 1)

            def exp_chunk(head, slot, c):
                js = CHUNKS[c]
                act.wait_ge(centred, head * T + js[-1] + 1)
                part = ring[:, slot, ROW_AT[js[0]]:ROW_AT[js[-1]] + ROW_W[js[-1]]]
                act.activation(part, part, ACT.Exp, scale=SCALE).then_inc(exped, 1)

            def copy_row(g, h, j, slot):
                n = (2 * g + h) * T + j
                act.wait_ge(row_done, n + 1)
                w = ROW_W[j]
                if w > BANK:
                    src = row_ps[:, j % 2, :].rearrange("p (c w) -> p c w", c=2)[:, :, 0:w // 2]
                    dst = row(slot, j).rearrange("p (c w) -> p c w", c=2)
                else:
                    src, dst = row_ps[:, j % 2, 0:w], row(slot, j)
                act.activation(dst, src, ACT.Copy).then_inc(row_copied, 1)

            def step(g, par):
                scores, queries_, vals, output = parts(g)
                a_slot, b_slot, old_b = 2 * par, 2 * par + 1, 2 * (1 - par) + 1
                if output:
                    act.wait_ge(att_done, g - 1)
                    act.wait_ge(summed, (2 * g - 2) * T)
                if scores:
                    for j in range(T):
                        copy_row(g, 0, j, a_slot)
                        if j == 3 and queries_:
                            rotary_weights(g + 1)
                if output:
                    act.wait_ge(att_scaled, g - 1)
                    act.activation(att_hi[:, :], att[:, :], ACT.Copy).then_inc(att_hi_set, 1)
                for j in range(T):
                    if scores:
                        copy_row(g, 1, j, b_slot)
                    if vals and j % 2 == 0:
                        exp_chunk(2 * g - 1, old_b, j // 2)
                if queries_:
                    latent_weights(g)
                    queries(g + 2, g, "f", q_hi)
                if scores:
                    for c in range(len(CHUNKS)):
                        exp_chunk(2 * g, a_slot, c)
                if vals:
                    o, _ = job(g, "n")
                    act.activation(n_hi[:, :], o, ACT.Copy).then_inc(n_hi_set, 1)

            for part, hi in enumerate((c1_hi, c2_hh)):
                for c in range(2):
                    o, _ = job(None, f"cq{part + 1}_{c}")
                    act.activation(hi[:, c * BANK:(c + 1) * BANK], o, ACT.Copy).then_inc(c_hi_set, 1)
            rotary_weights(0)
            queries(0, None, "k", key_hi)
            for c in range(2):
                o, read = job(None, f"v_{c}")
                act.activation(values[:, 4 * c:4 * c + 4, :], o[:, 0:4 * R].rearrange("p (i r) -> p i r", i=4), ACT.Copy
                               ).then_inc(read, 2)
            latent_weights(None)
            queries(1, None, "f", q_hi)
            run_steps(act, step)

            act.wait_ge(mean_linked, 2 * T + 1)
            act.activation(thin[0], moments[:, :, 1], ACT.Sqrt, bias=eps_sb).then_inc(spread_ready, 1)
            for i in range(T):
                act.wait_ge(x1_turned, i + 1)
                act.activation(x1T[:, :, i * P:(i + 1) * P], job_ps[:, i % 2, :].rearrange("p (k s) -> p k s", k=KD),
                               ACT.Copy).then_inc(x1T_set, 1)
            act.wait_ge(logits_centred, 1)
            act.activation(small[1], small[0], ACT.Exp).then_inc(logits_exped, 1)
            for c in range(2):
                act.wait_ge(hw_turned, c + 1)
                act.activation(hT[:, c * BANK:(c + 1) * BANK], row_ps[:, 1, c * BANK:(c + 1) * BANK], ACT.Copy
                               ).then_inc(hT_set, 1)
            for i in range(T):
                act.wait_ge(var_ready, i + 1)
                act.activation(thin[8][:, i:i + 1], moments[:, i, 1:2], ACT.Sqrt, bias=eps_sb).then_inc(sd_ready, 1)

        @block.gpsimd
        def _(pool):
            def rotary_weights(g):
                pool.wait_ge(st_rot_hi, 2 * g + 1)
                if isinstance(g, int) and g == 0:
                    pool.wait_ge(ld_qw, UNF)
                pool.tensor_tensor(rot_cols(st1_lo[:, :]), wr1.rearrange("p (a b) -> p a b", a=2),
                                   rot_cols(st1_hi[:, :].bitcast(F32)), ALU.subtract).then_inc(st_rot_lo, 1)
                pool.wait_ge(st_rot_hi, 2 * g + 2)
                pool.wait_ge(st_rot_lo, 2 * g + 1)
                low = slice(R, P)
                pool.tensor_tensor(rot_cols(st2[low, :]), wr2[low, :].rearrange("p (a b) -> p a b", a=2),
                                   rot_cols(st2[low, :].bitcast(F32)), ALU.subtract).then_inc(st_rot_lo, 1)
                pool.wait_ge(st_rot_lo, 2 * g + 2)

            def queries(n, hi, lo):
                for c in range(2):
                    for h in range(2):
                        if h == 1:
                            pool.wait_ge(fused_set, 4 * n + 2 * c + 1)
                        elif c == 1 or not isinstance(n, int) or n > 0:
                            pool.wait_ge(qk_lo_set, 4 * n + 2 * c)
                        pool.wait_ge(rot_set, 4 * n + 2 * c + h + 1)
                        rot = slice(R * (1 - h), R * (1 - h) + R)
                        pool.tensor_tensor(fused[rot, h, :], fused[rot, h, :], turned[rot, :], ALU.add
                                           ).then_inc(fused_set, 1)
                    pool.wait_ge(fused_set, 4 * n + 2 * c + 2)
                    for h in range(2):
                        pool.wait_ge(qk_hi_set, 4 * n + 2 * c + h + 1)
                        cols = slice(c * BANK, (c + 1) * BANK)
                        pool.tensor_tensor(lo[:, h, cols], fused[:, h, :], hi[:, h, cols].bitcast(F32), ALU.subtract
                                           ).then_inc(qk_lo_set, 1)

            def sum_head(head, h, slot, prev):
                acc = psum_p[:, h, :]
                if prev is not None:
                    pool.wait_ge(job_done, prev)
                for j in range(1, T):
                    pool.wait_ge(exped, head * len(CHUNKS) + CHUNK_OF[j] + 1)
                    if j > 1:
                        pool.wait_ge(summed, head * T + j)
                    before = row(slot, 0)[:, P:] if j == 1 else acc[:, P * j:]
                    pool.tensor_tensor(acc[:, P * j:], before, row(slot, j), ALU.add).then_inc(summed, 1)
                    if j == 1:
                        pool.tensor_copy(acc[:, 0:P], row(slot, 0)[:, 0:P]).then_inc(summed, 1)

            def step(g, par):
                scores, queries_, vals, output = parts(g)
                if queries_:
                    rotary_weights(g + 1)
                if output:
                    pool.wait_ge(att_hi_set, g - 1)
                    pool.tensor_tensor(att_lo[:, :], att[:, :], att_hi[:, :].bitcast(F32), ALU.subtract
                                       ).then_inc(att_lo_set, 1)
                if vals:
                    prev = None
                    if output:
                        prev = Job(g - 1, "lb_1").done if isinstance(g, int) else \
                            Job(g, "lb_1").done - JOBS_PER_STEP
                    sum_head(2 * g - 1, 1, 2 * (1 - par) + 1, prev)
                    pool.wait_ge(summed, 2 * g * T)
                if queries_:
                    queries(g + 2, q_hi, q_lo)
                if scores:
                    sum_head(2 * g, 0, 2 * par, Job(g, "la_1").done if vals else None)

            rotary_weights(0)
            queries(0, key_hi, key_lo)
            queries(1, q_hi, q_lo)
            run_steps(pool, step)

            pool.wait_ge(ld_ffn, 3 * UNF)
            for i in range(T):
                pool.wait_ge(x1_set, i + 1)
                pool.tensor_tensor(res[:, i, :], y[:, i, :], bias_sb, ALU.add).then_inc(x1b_set, 1)

        @block.vector
        def _(dve):
            def job(g, name):
                j = Job(g, name)
                dve.wait_ge(job_done, j.done)
                return job_ps[:, j.bank, :], job_read[j.bank]

            def latent_weights(n, step_g):
                o, read = job(step_g, "m")
                dve.wait_ge(st_lat_hi, 2 * n + 2)
                low = slice(R, P)
                dve.tensor_tensor(lat_cols(st2[low, :]), o[low, P:2 * P].rearrange("p (a b) -> p a b", a=2),
                                  lat_cols(st2[low, :].bitcast(F32)), ALU.subtract).then_inc(st_lat_lo, 1)
                dve.tensor_tensor(lat_cols(st1_lo[:, :]), o[:, 0:P].rearrange("p (a b) -> p a b", a=2),
                                  lat_cols(st1_hi[:, :].bitcast(F32)), ALU.subtract).then_inc(read, 2)

            def queries(n, step_g, kind):
                for c in range(2):
                    cols = slice(c * BANK, (c + 1) * BANK)
                    o, read = job(step_g, f"{kind}z_{c}")
                    if c > 0 or not isinstance(n, int) or n > 0:
                        dve.wait_ge(fused_set, 4 * n + 2 * c)
                    dve.tensor_tensor(turned[:, :], o, cos_sin[:, 1, cols], ALU.mult).then_inc(read, 2)
                    for h in range(2):
                        rot = slice(R * (1 - h), R * (1 - h) + R)
                        o, read = job(step_g, f"{kind}{'ab'[h]}_{c}")
                        if c > 0 or not isinstance(n, int) or n > 0:
                            dve.wait_ge(qk_lo_set, 4 * n + 2 * c + h - 1)
                        dve.tensor_tensor(fused[rot, h, :], o[rot, :], cos_sin[rot, 0, cols], ALU.mult
                                          ).then_inc(rot_set, 1)

            def max_row(g, h, j, slot):
                n = (2 * g + h) * T + j
                acc = top[:, h, :]
                dve.wait_ge(row_copied, n + 1)
                if j == 0:
                    dve.tensor_copy(acc[:, 0:P], row(slot, 0)[:, 0:P]).then_inc(row_maxed, 1)
                    return
                if j > 1:
                    dve.wait_ge(row_maxed, n)
                before = row(slot, 0)[:, P:] if j == 1 else acc[:, P * j:]
                dve.tensor_tensor(acc[:, P * j:], before, row(slot, j), ALU.max).then_inc(row_maxed, 1)

            def centre_row(head, h, j, slot):
                if j == 0:
                    dve.wait_ge(max_loaded[h], (head + 2 - h) * (UNF // 2))
                    dve.wait_ge(row_copied, (head + 1) * T)
                r = row(slot, j)
                dve.tensor_tensor(r, r, maxes[:, h, P * j:], ALU.subtract).then_inc(centred, 1)

            def reduce_turned(g, kind, h, col, op):
                for c in range(2):
                    o, read = job(g, f"{kind}{'ab'[h]}_{c}")
                    dve.tensor_reduce(col[:, h, 4 * c:4 * c + 4], o.rearrange("p (i t) -> p i t", i=4), AX_X, op
                                      ).then_inc(read, 2)

            def invert(g, h):
                for c in range(2):
                    j = Job(g, f"l{'ab'[h]}_{c}")
                    dve.wait_ge(job_read[j.bank], j.read)
                dve.reciprocal(inv_col[:, h, :], sum_col[:, h, :]).then_inc(inv_ready, 1)

            def add_output(g, lo, hi):
                for i in range(lo, hi):
                    o, read = job(g, f"o_{i}")
                    dve.tensor_tensor(y[:, i, :], y[:, i, :], o, ALU.add).then_inc(read, 2)

            def step(g, par):
                scores, queries_, vals, output = parts(g)
                a_slot, b_slot, old_b = 2 * par, 2 * par + 1, 2 * (1 - par) + 1
                for j in range(T):
                    if scores:
                        max_row(g, 0, j, a_slot)
                    if vals:
                        centre_row(2 * g - 1, 1, j, old_b)
                    if output and j == 2:
                        dve.wait_ge(att_done, g - 1)
                        dve.wait_ge(inv_loaded, (g - 1) * 2 * UNF)
                        dve.tensor_tensor(att[:, :], att[:, :], att_ps[:, :, :].rearrange("p c n -> p (c n)"), ALU.mult
                                          ).then_inc(att_scaled, 1)
                if scores:
                    for j in range(T):
                        max_row(g, 1, j, b_slot)
                        if j == 4:
                            reduce_turned(g, "t", 0, max_col, ALU.max)
                if queries_:
                    latent_weights(g + 1, g)
                if output:
                    add_output(g, 0, 4)
                if scores:
                    reduce_turned(g, "t", 1, max_col, ALU.max)
                if queries_:
                    queries(g + 2, g, "f")
                if output:
                    add_output(g, 4, 8)
                if vals:
                    reduce_turned(g, "l", 0, sum_col, ALU.add)
                    invert(g, 0)
                if scores:
                    for j in range(T):
                        centre_row(2 * g, 0, j, a_slot)
                if vals:
                    o, read = job(g, "n")
                    dve.wait_ge(n_hi_set, g)
                    dve.tensor_tensor(n_lo[:, :], o, n_hi[:, :].bitcast(F32), ALU.subtract).then_inc(read, 2)
                    reduce_turned(g, "l", 1, sum_col, ALU.add)
                    invert(g, 1)

            n = 0
            for part, (hi, lo) in enumerate(((c1_hi, c1_lo), (c2_hh, c2_lo))):
                for c in range(2):
                    o, read = job(None, f"cq{part + 1}_{c}")
                    n += 1
                    dve.wait_ge(c_hi_set, n)
                    rows = slice(0, P if part == 0 else R)
                    cols = slice(c * BANK, (c + 1) * BANK)
                    dve.tensor_tensor(lo[rows, cols], o[rows, :], hi[rows, cols].bitcast(F32), ALU.subtract
                                      ).then_inc(read, 2)
            dve.wait_ge(ld_tab, UNF)
            queries(0, None, "k")
            latent_weights(0, None)
            queries(1, None, "f")
            dve.wait_ge(ld_y, UNF)
            run_steps(dve, step)

            linked = [0]

            def link(ins):
                linked[0] += 1
                ins.then_inc(mean_linked, 1)
                dve.wait_ge(mean_linked, linked[0])

            for n in range(2):
                dve.wait_ge(job_read[n], LAST_READ[n])
            link(dve.memset(eps_sb, EPS))
            for i in range(T):
                link(dve.bn_stats(stats[:, i, :], y[:, i, :]))
            for i in range(T):
                link(dve.bn_aggr(moments[:, i, :], stats[:, i, :]))
            dve.wait_ge(spread_ready, 1)
            link(dve.reciprocal(thin[1], thin[0]))
            for i in range(T):
                dve.tensor_scalar(y[:, i, :], y[:, i, :], moments[:, i, 0:1], thin[1][:, i:i + 1], ALU.subtract, ALU.mult
                                  ).then_inc(x1_set, 1)
            for i in range(T):
                dve.wait_ge(hr_done, i + 1)
                dve.tensor_copy(hr[:, i, :], row_ps[:, (i % 4) // 2, (i % 2) * BANK:(i % 2) * BANK + HW]).then_inc(hr_set, 1)
            dve.wait_ge(hr_set, T)

            def over(t):
                return t.unsqueeze(2).broadcast_to([P, T, NE])

            logits = hr[:, :, NE * RANK:]
            centred_l, probs, is_top, ranked, first, rest, second, weight = small
            top1, total, inv_total, at1, top2, at2 = thin[2:8]
            link(dve.tensor_reduce(top1, logits, AX_X, ALU.max))
            dve.tensor_tensor(centred_l, logits, over(top1), ALU.subtract).then_inc(logits_centred, 1)
            dve.wait_ge(logits_exped, 1)
            link(dve.tensor_reduce(total, probs, AX_X, ALU.add))
            link(dve.reciprocal(inv_total, total))
            link(dve.tensor_tensor(probs, probs, over(inv_total), ALU.mult))

            dve.wait_ge(ld_ffn, 3 * UNF)

            def take_largest(values_, largest, place, chosen):
                link(dve.tensor_reduce(largest, values_, AX_X, ALU.max))
                link(dve.tensor_tensor(is_top, values_, over(largest), ALU.is_equal))
                link(dve.tensor_tensor(ranked, is_top, rank_sb, ALU.mult))
                link(dve.tensor_reduce(place, ranked, AX_X, ALU.max))
                link(dve.tensor_tensor(chosen, rank_sb, over(place), ALU.is_equal))

            take_largest(probs, top1, at1, first)
            link(dve.scalar_tensor_tensor(out=rest, in0=first, scalar=-2.0, in1=probs, op0=ALU.mult, op1=ALU.add))
            take_largest(rest, top2, at2, second)
            link(dve.tensor_tensor(weight, first, second, ALU.add))
            link(dve.tensor_tensor(weight, weight, probs, ALU.mult))
            link(dve.tensor_tensor(total, top1, top2, ALU.add))
            link(dve.reciprocal(inv_total, total))
            link(dve.scalar_tensor_tensor(out=weight, in0=weight, scalar=LORA_SCALE, in1=over(inv_total),
                                          op0=ALU.mult, op1=ALU.mult))
            for i in range(T):
                ins = dve.tensor_tensor(hw[:, i, :].rearrange("p (e r) -> p e r", e=NE),
                                        hr[:, i, 0:NE * RANK].rearrange("p (e r) -> p e r", e=NE),
                                        weight[:, i, :].unsqueeze(2).broadcast_to([P, NE, RANK]), ALU.mult)
            ins.then_inc(hw_set, 1)

            rows = [row_ps[:, n // 2, (n % 2) * BANK:(n % 2 + 1) * BANK] for n in range(4)]
            ff_banks = ffn_banks(rows, [job_ps[:, n, :] for n in range(2)])

            def finish(i):
                dve.wait_ge(sd_ready, i + 1)
                link(dve.reciprocal(thin[9][:, i:i + 1], thin[8][:, i:i + 1]))
                dve.tensor_scalar(res[:, i, :], res[:, i, :], moments[:, i, 0:1], thin[9][:, i:i + 1],
                                  ALU.subtract, ALU.mult).then_inc(res_set, 1)

            for i in range(T):
                dve.wait_ge(x1b_set, i + 1)
                dve.wait_ge(ff_done, i + 1)
                link(dve.tensor_tensor(res[:, i, :], res[:, i, :], ff_banks[i], ALU.add))
                link(dve.bn_stats(stats[:, i, :], res[:, i, :]))
                dve.bn_aggr(moments[:, i, :], stats[:, i, :]).then_inc(var_ready, 1)
                if i > 0:
                    finish(i - 1)
            finish(T - 1)


def kernel(**inputs):
    import numpy as np
    import concourse.bacc as bacc
    from concourse import mybir as mb
    from concourse.bass_utils import run_bass_kernel_spmd

    def get(name):
        return np.asarray(inputs[name])

    def tiles(a):
        return np.ascontiguousarray(a.reshape(-1, 128, a.shape[-1]).transpose(1, 0, 2))

    def swap(a):
        return np.concatenate([a[..., 32:], a[..., :32]], -1)

    x = get("L0_attn_hidden_states")[0]
    w_qd = get("L0_attn_w_q_down")
    w_kv, w_kr = get("L0_attn_w_kv_down"), get("L0_attn_w_k_rope")
    nope = get("L0_attn_w_q_up_nope").reshape(192, 32, 128).transpose(1, 2, 0)
    nope = np.concatenate([nope, nope[:, :, 128:]], -1)
    nope = nope.reshape(16, 2, 128, 256).transpose(0, 2, 1, 3).reshape(16, 128, 512)
    uk = get("L0_attn_w_uk").reshape(16, 2, 128, 64).transpose(0, 2, 1, 3).reshape(16, 128, 128)
    rope = get("L0_attn_w_q_up_rope").reshape(192, 16, 2, 64).transpose(1, 0, 2, 3)
    rot = np.concatenate([swap(rope[:, :, 1]), swap(rope[:, :, 0]), rope[:, :, 0], rope[:, :, 1]], -1)
    qw = np.concatenate([nope, uk, rot[:, 0:128], np.concatenate([rot[:, 128:], rot[:, 128:]], 1)], -1)
    uv = get("L0_attn_w_uv").reshape(16, 2, 128, 64).transpose(0, 2, 1, 3).reshape(16, 128, 128)
    wo = get("L0_attn_w_out").reshape(16, 2, 128, 512).transpose(0, 2, 1, 3).reshape(16, 128, 1024)

    f32 = np.float32
    freqs = f32(1.0) / f32(10000.0) ** (np.arange(0, 64, 2, dtype=f32) / f32(64))
    ramp = np.clip((f32(2.0 * np.pi) / freqs / f32(4096.0) - f32(1.0)) / f32(31.0), f32(0), f32(1))
    inv_freq = freqs / (f32(1.0) - ramp + ramp * f32(40.0))
    angle = (np.arange(1024, dtype=f32)[:, None] * inv_freq[None, :]).T
    cos, sin = np.cos(angle), np.sin(angle)
    tables = np.stack([np.tile(cos, (4, 1)), np.concatenate([-sin, sin, -sin, sin], 0)], 1).astype(f32)

    import ml_dtypes
    t = np.arange(128)
    arrays = {
        "in_xT": np.ascontiguousarray(tiles(np.ascontiguousarray(x.T))),
        "in_x": x,
        "in_wq_down": tiles(np.concatenate([w_qd, w_qd[:, 128:]], -1)),
        "in_wk": tiles(np.concatenate([swap(w_kr), swap(w_kr), w_kv, w_kr, w_kr, w_kv], -1)),
        "in_qw": qw, "in_ow": np.concatenate([uv, wo], -1),
        "in_tables": tables,
        "in_ident": np.eye(128, dtype=f32),
        "in_ident16": np.eye(128, dtype=f32).astype(ml_dtypes.bfloat16),
        "in_mask16": np.where(t[None, :] < t[:, None], f32(-3e38), f32(0)).astype(ml_dtypes.bfloat16),
        "in_rank": np.tile(np.arange(8, 0, -1).astype(f32), (128, 8)),
        "in_ffn": np.concatenate([
            tiles(get("L0_ffn_W_base").T).reshape(128, -1),
            tiles(np.concatenate([get("L0_ffn_A").reshape(128, 512).T, get("L0_ffn_W_router").T], -1)).reshape(128, -1),
            get("L0_ffn_B").transpose(0, 2, 1).reshape(128, 512)], -1),
        "in_bias": get("L0_ffn_b_base")[None, :],
    }
    arrays = {k: np.ascontiguousarray(v) for k, v in arrays.items()}
    nc = bacc.Bacc("TRN2", target_bir_lowering=False, num_devices=1)
    args = [nc.dram_tensor(k, v.shape, mb.dt.from_np(v.dtype), kind="ExternalInput").ap() for k, v in arrays.items()]
    out = nc.dram_tensor("out", (1024, 512), mb.dt.float32, kind="ExternalOutput").ap()
    build(nc, *args, out)
    r = run_bass_kernel_spmd(nc, [arrays], core_ids=[0])
    return r.results[0]["out"].reshape(1, 1024, 512)
```

```python
from contextlib import ExitStack

import concourse.bass as bass
from concourse import mybir

F32 = mybir.dt.float32
F32R = mybir.dt.float32r
BF16 = mybir.dt.bfloat16
ALU = mybir.AluOpType
ACT = mybir.ActivationFunctionType
AX_X = mybir.AxisListType.X

P = 128
S = 1024
D = 512
H = 32
QL = 192
R = 64
DN = 128
PAIRS = H // 2
T = S // P
KD = D // P
BANK = 512
NE, RANK = 8, 16
LORA_SCALE = 32 / RANK
EPS = 1e-5
SCALE = float(1.0 / (DN + R) ** 0.5)

ROW_W = [S - P * j for j in range(T)]
ROW_AT = [sum(ROW_W[:j]) for j in range(T)]
HEAD_COLS = sum(ROW_W)
CHUNKS = [(0,), (1, 2), (3, 4), (5, 6, 7)]
EARLY_ROWS = 5
EXP_B = {(0, 1): 0, (0, 4): 1, (1, 2): 2, (1, 6): 3}
CHUNK_OF = [c for j in range(T) for c in range(len(CHUNKS)) if j in CHUNKS[c]]

Z_AT, A_AT, B_AT, ST_W = 0, 128, 256, 384
LB_AFTER = 0
UNF = 16

BANKS = 6
PRE = [f"cq{part}_{c}" for part in (1, 2) for c in range(2)] + [f"k{n}_{c}" for c in range(2) for n in "zab"] \
    + ["v_0", "v_1", "m"] + [f"f{n}_{c}" for c in range(2) for n in "zab"]


def step_uses(g):
    s, f, p, o = g < PAIRS, g + 1 < PAIRS, 1 <= g <= PAIRS, g >= 2
    uses = []
    if s:
        uses += [f"row{h}{j}" for h in range(2) for j in range(T)]
    if f:
        uses += ["m"]
    if p:
        uses += ["la_0", "la_1"]
    if o:
        uses += [f"o_{i}" for i in range(4)]
    if s:
        uses += ["ta_0", "ta_1", "tb_0", "tb_1"]
    if f:
        uses += [f"f{n}_0" for n in "zab"]
    if o:
        uses += [f"o_{i}" for i in range(4, 8)]
    if f:
        uses += [f"f{n}_1" for n in "zab"]
    if p:
        uses += ["n", "lb_0", "lb_1"]
    return uses


def reader(name):
    if name.startswith("row"):
        return "row"
    return "act" if name[:2] in ("ka", "kb", "fa", "fb") or name[0] == "v" else "dve"


STEPS = PAIRS + 2
STEADY = 2
LOOP = (STEADY + 1, PAIRS - 3)


def plan():
    written, reads = {"row": 0, "job": 0}, {"row": 0, "act": 0, "dve": 0}
    holds = [None] * BANKS
    table = {}
    for g in [None, *range(STEPS)]:
        bank = 0
        for name in PRE if g is None else step_uses(g):
            wide = name.startswith("row") and ROW_W[int(name[-1])] > BANK
            if wide and bank % 2:
                bank += 1
            banks = [bank % BANKS] + [bank % BANKS + 1] * wide
            bank += 1 + wide
            who = reader(name)
            kind = "row" if who == "row" else "job"
            written[kind] += 1
            reads[who] += 1
            before = sorted({holds[b] for b in banks if holds[b]}, key=str)
            table[g, name] = (banks, written[kind], reads[who], before)
            for b in banks:
                holds[b] = (who, g, name)
    return table, dict(reads)


PLAN, ALL_READS = plan()
GROWTH = {who: sum(reader(u) == who for u in step_uses(STEADY)) for who in ("row", "act", "dve")}
GROWTH["job"] = GROWTH["act"] + GROWTH["dve"]


class Use:

    def __init__(self, g, name, back=0):
        fixed = g is None or isinstance(g, int)
        at = g if g is None else g - back if fixed else STEADY
        extra = None if fixed else g - (STEADY + back)
        self.banks, done, read, self.before = PLAN[at, name]
        self.bank = self.banks[0]
        self.who = reader(name)
        self.step, self.at = g, at
        kind = "row" if self.who == "row" else "job"
        self.done = done if fixed else extra * GROWTH[kind] + done
        self.read = read if fixed else extra * GROWTH[self.who] + read

    def frees(self):
        for who, g, name in self.before if self.step is None or isinstance(self.step, int) else \
                PLAN[STEADY + 1, self.name_of()][3]:
            if self.step is None or isinstance(self.step, int):
                yield who, Use(g, name).read
            else:
                yield who, Use(self.step, name, back=STEADY + 1 - g).read

    def name_of(self):
        return next(n for (g, n), v in PLAN.items() if g == self.at and v[0] is self.banks)


def build(nc, xT, xres, wq_down, wk, qw, ow, tables, ident, ident16, mask16, rank_tab, ffn_w, bias, out):
    with ExitStack() as ctx:
        def sb(name, shape, dt=F32):
            return ctx.enter_context(nc.sbuf_tensor(name, shape, dt))

        def ps(name, shape, dt=F32):
            return ctx.enter_context(nc.psum_tensor(name, shape, dt))

        def sem(name):
            return ctx.enter_context(nc.semaphore(name))

        ring = sb("ring", [P, 4, HEAD_COLS])
        key_hi = sb("key_hi", [P, 2, S], F32R)
        key_lo = sb("key_lo", [P, 2, S], F32R)
        q_hi = sb("q_hi", [P, 2, S], F32R)
        q_lo = sb("q_lo", [P, 2, S], F32R)
        turned = sb("turned", [P, BANK])
        fused = sb("fused", [P, 2, BANK])
        cos_sin = sb("cos_sin", [P, 2, S])
        c1_hi = sb("c1_hi", [P, S], F32R)
        c1_lo = sb("c1_lo", [P, S], F32R)
        c2_hh = sb("c2_hh", [P, S], F32R)
        c2_lo = sb("c2_lo", [R, S], F32R)
        top = sb("top", [P, 2, S])
        psum_p = sb("psum_p", [P, 2, S])
        maxes = sb("maxes", [P, 2, S])
        att = sb("att", [P, S])
        att_hi = sb("att_hi", [P, S], F32R)
        att_lo = sb("att_lo", [P, S], F32R)
        n_hi = sb("n_hi", [P, D], F32R)
        n_lo = sb("n_lo", [P, D], F32R)
        qw_sb = sb("qw_sb", [P, 2 * 256 + 2 * R + 512])
        ow_sb = sb("ow_sb", [P, 2 * R + 2 * D])
        st1_hi = sb("st1_hi", [P, ST_W], F32R)
        st1_lo = sb("st1_lo", [P, ST_W], F32R)
        st2 = sb("st2", [P, ST_W], F32R)
        y = sb("y", [P, T, D])
        values = sb("values", [P, T, R])
        id32 = sb("id32", [P, P])
        id16 = sb("id16", [P, P], BF16)
        causal16 = sb("causal16", [P, P], BF16)
        max_col = sb("max_col", [P, 2, T])
        sum_col = sb("sum_col", [P, 2, T])
        inv_col = sb("inv_col", [P, 2, T])

        bank_ps = ps("bank_ps", [P, BANKS, BANK])
        att_ps = ps("att_ps", [P, 2, BANK])

        max_dram = nc.dram_tensor("max_rows", (2, S), F32, kind="Internal").ap()
        inv_dram = nc.dram_tensor("inv_rows", (2, S), F32, kind="Internal").ap()

        def row(slot, j):
            return ring[:, slot, ROW_AT[j]:ROW_AT[j] + ROW_W[j]]

        flat = ring[:, :, :].rearrange("p a n -> p (a n)")
        at = [0]

        def carve(n):
            at[0] += n
            return flat[:, at[0] - n:at[0]]

        xT_sb = carve(KD * S).rearrange("p (k s) -> p k s", k=KD)
        wqd_sb = carve(KD * 256).rearrange("p (k n) -> p k n", k=KD)
        wk_sb = carve(KD * 384).rearrange("p (k n) -> p k n", k=KD)
        assert at[0] <= 2 * HEAD_COLS
        at[0] = 0
        HW = NE * RANK + NE
        base_w = carve(KD * D).rearrange("p (k n) -> p k n", k=KD)
        hr_w = carve(KD * HW).rearrange("p (k n) -> p k n", k=KD)
        up_w = carve(D)
        bias_sb = carve(D)
        rank_sb = carve(T * NE).rearrange("p (i e) -> p i e", e=NE)
        ffn_loaded_cols = at[0]
        x1T = carve(KD * S).rearrange("p (k s) -> p k s", k=KD)
        assert at[0] <= 2 * HEAD_COLS
        at[0] = 2 * HEAD_COLS
        hr = carve(T * HW).rearrange("p (i n) -> p i n", i=T)
        hT = carve(S)
        small = [carve(T * NE).rearrange("p (i e) -> p i e", e=NE) for _ in range(8)]
        thin = [carve(T) for _ in range(10)]
        stats = carve(T * 6).rearrange("p (i n) -> p i n", i=T)
        moments = carve(T * 2).rearrange("p (i n) -> p i n", i=T)
        eps_sb = carve(1)
        hw = carve(T * P).rearrange("p (i n) -> p i n", i=T)
        res = carve(T * D).rearrange("p (i n) -> p i n", i=T)
        assert at[0] <= 4 * HEAD_COLS

        qnT = [qw_sb[:, h * 256:(h + 1) * 256] for h in range(2)]
        wuk = [qw_sb[:, 512 + h * R:512 + (h + 1) * R] for h in range(2)]
        wr1 = qw_sb[:, 640:896]
        wr2 = qw_sb[:, 896:1152]
        wuv = [ow_sb[:, h * R:(h + 1) * R] for h in range(2)]
        wout = [ow_sb[:, 128 + h * D:128 + (h + 1) * D] for h in range(2)]

        def rot_cols(t):
            return t.rearrange("p (a b) -> p a b", b=192)[:, :, 0:128]

        def lat_cols(t):
            return t.rearrange("p (a b) -> p a b", b=192)[:, :, 128:192]

        ld_cq = sem("ld_cq")
        ld_k = sem("ld_k")
        ld_tab = sem("ld_tab")
        ld_id = sem("ld_id")
        ld_y = sem("ld_y")
        ld_qw = sem("ld_qw")
        ld_ow = sem("ld_ow")
        ld_ffn = sem("ld_ffn")
        max_written = sem("max_written")
        max_loaded = [sem("max_loaded_a"), sem("max_loaded_b")]
        inv_written = sem("inv_written")
        inv_loaded = sem("inv_loaded")
        job_done = sem("job_done")
        dve_read = sem("dve_read")
        act_read = sem("act_read")
        row_done = sem("row_done")
        row_copied = sem("row_copied")
        row_maxed = sem("row_maxed")
        centred = sem("centred")
        exped = sem("exped")
        summed = sem("summed")
        inv_ready = sem("inv_ready")
        att_done = sem("att_done")
        att_scaled = sem("att_scaled")
        att_hi_set = sem("att_hi_set")
        att_lo_set = sem("att_lo_set")
        n_hi_set = sem("n_hi_set")
        c_hi_set = sem("c_hi_set")
        rot_set = sem("rot_set")
        fused_set = sem("fused_set")
        qk_hi_set = sem("qk_hi_set")
        qk_lo_set = sem("qk_lo_set")
        st_rot_hi = sem("st_rot_hi")
        st_rot_lo = sem("st_rot_lo")
        st_lat_hi = sem("st_lat_hi")
        st_lat_lo = sem("st_lat_lo")
        y_set = sem("y_set")
        mean_linked = sem("mean_linked")
        spread_ready = sem("spread_ready")
        x1_set = sem("x1_set")
        x1_turned = sem("x1_turned")
        x1T_set = sem("x1T_set")
        hr_done = sem("hr_done")
        hr_set = sem("hr_set")
        logits_centred = sem("logits_centred")
        logits_exped = sem("logits_exped")
        hw_set = sem("hw_set")
        hw_turned = sem("hw_turned")
        hT_set = sem("hT_set")
        ff_done = sem("ff_done")
        x1b_set = sem("x1b_set")
        var_ready = sem("var_ready")
        sd_ready = sem("sd_ready")
        res_set = sem("res_set")
        out_written = sem("out_written")

        read_by = {"row": row_copied, "act": act_read, "dve": dve_read}

        def run_steps(eng, step):
            for g in range(LOOP[0]):
                step(g, g % 2)
            with eng.Fori(LOOP[0], LOOP[1], 2) as g:
                step(g, LOOP[0] % 2)
                step(g + 1, 1 - LOOP[0] % 2)
            for g in range(LOOP[1], STEPS):
                step(g, g % 2)

        def ffn_banks(rows, jobs):
            return [att_ps[:, 0, :], att_ps[:, 1, :], *jobs, *rows]

        def parts(g):
            if not isinstance(g, int):
                return True, True, True, True
            return g < PAIRS, g + 1 < PAIRS, 1 <= g <= PAIRS, g >= 2

        block = ctx.enter_context(nc.Block())

        @block.sync
        def _(sp):
            sp.dma_start(wqd_sb, wq_down).then_inc(ld_cq, 16)
            for k in range(KD):
                sp.dma_start(xT_sb[:, k, :], xT[:, k, :]).then_inc(ld_cq, 16)
            sp.dma_start(wk_sb, wk).then_inc(ld_k, 16)
            sp.dma_start(cos_sin[:, :, :], tables).then_inc(ld_tab, 16)
            sp.dma_start(qw_sb[:, :], qw[0, :, :]).then_inc(ld_qw, 16)
            sp.dma_start(id32[:, :], ident).then_inc(ld_id, 16)
            sp.dma_start(id16[:, :], ident16).then_inc(ld_id, 16)
            sp.dma_start(causal16[:, :], mask16).then_inc(ld_id, 16)
            sp.dma_start(ow_sb[:, :], ow[0, :, :]).then_inc(ld_ow, 16)
            sp.dma_start(y[:, :, :], xres.rearrange("(i p) d -> p i d", p=P)).then_inc(ld_y, 16)

            def values_of(*targets):
                return [t if isinstance(t, int) else sp.to_reg(t) for t in targets]

            def maxima(g, h):
                reduced, written, used = values_of(Use(g, f"t{'ab'[h]}_1").read,
                                                   (2 * g + h + 1) * UNF, (2 * g + h - 1) * T)
                sp.wait_ge(dve_read, reduced)
                sp.dma_start(max_dram[h, :].rearrange("(p i) -> p i", i=T), max_col[:, h, :]).then_inc(max_written, 16)
                sp.wait_ge(max_written, written)
                if not isinstance(g, int) or g > 0:
                    sp.wait_ge(centred, used)
                sp.dma_start(maxes[:, h, :], max_dram[h:h + 1, :].partition_broadcast(P).rearrange("p a s -> p (a s)")
                             ).then_inc(max_loaded[h], 16)

            def step(g, par):
                scores, queries, vals, _ = parts(g)
                if queries:
                    sp.wait_ge(st_lat_lo, g + 1)
                    sp.wait_ge(st_rot_hi, 2 * g + 2)
                    sp.wait_ge(st_rot_lo, 2 * g + 2)
                    src = qw[g + 1, :, :] if isinstance(g, int) else qw[bass.ds(g + 1, 1), :, :].rearrange("a p n -> p (a n)")
                    sp.dma_start(qw_sb[:, :], src).then_inc(ld_qw, 16)
                if scores:
                    maxima(g, 0)
                    maxima(g, 1)
                if vals:
                    ready0, ready1, written, split, n_made = values_of(2 * g - 1, 2 * g, g * (2 * UNF), g - 1, g)
                    sp.wait_ge(inv_ready, ready0)
                    sp.dma_start(inv_dram[0, :].rearrange("(p i) -> p i", i=T), inv_col[:, 0, :]).then_inc(inv_written, 16)
                    sp.wait_ge(inv_ready, ready1)
                    sp.dma_start(inv_dram[1, :].rearrange("(p i) -> p i", i=T), inv_col[:, 1, :]).then_inc(inv_written, 16)
                    if not isinstance(g, int) or g > 1:
                        sp.wait_ge(att_lo_set, split)
                    sp.wait_ge(inv_written, written)
                    for h in range(2):
                        sp.dma_start(att[R * h:R * h + R, :],
                                     inv_dram[h:h + 1, :].partition_broadcast(R).rearrange("p a s -> p (a s)")
                                     ).then_inc(inv_loaded, 16)
                    if scores:
                        sp.wait_ge(n_hi_set, g)
                        src = ow[g, :, :] if isinstance(g, int) else ow[bass.ds(g, 1), :, :].rearrange("a p n -> p (a n)")
                        sp.dma_start(ow_sb[:, :], src).then_inc(ld_ow, 16)
                if isinstance(g, int) and g == PAIRS:
                    sp.wait_ge(att_done, PAIRS - 1)
                    sp.wait_ge(summed, 2 * T * (PAIRS - 1))
                    n = KD * D + KD * HW + D
                    sp.dma_start(flat[:, 0:n], ffn_w).then_inc(ld_ffn, 16)
                    sp.dma_start(bias_sb, bias.partition_broadcast(P).rearrange("p a s -> p (a s)")).then_inc(ld_ffn, 16)
                    sp.dma_start(flat[:, n + D:n + D + T * NE], rank_tab).then_inc(ld_ffn, 16)

            run_steps(sp, step)
            for i in range(T):
                sp.wait_ge(res_set, i + 1)
                sp.dma_start(out[i * P:(i + 1) * P, :], res[:, i, :]).then_inc(out_written, 16)
            sp.wait_ge(out_written, 16 * T)

        @block.tensor
        def _(pe):
            def open_use(g, name):
                use = Use(g, name)
                for who, count in use.frees():
                    pe.wait_ge(read_by[who], count)
                return use

            def open_job(g, name):
                return bank_ps[:, open_use(g, name).bank, :]

            def queries(g, step_g, chunks):
                if 0 in chunks:
                    pe.wait_ge(st_rot_hi, 2 * g + 2)
                    pe.wait_ge(st_rot_lo, 2 * g + 2)
                    pe.wait_ge(st_lat_hi, 2 * g + 2)
                    pe.wait_ge(st_lat_lo, g + 1)
                    pe.wait_ge(dve_read, Use(step_g, "m").read)
                for c in chunks:
                    s0, s1 = c * BANK, (c + 1) * BANK
                    for name, col in (("z", Z_AT), ("a", A_AT), ("b", B_AT)):
                        o = open_job(step_g, f"f{name}_{c}")
                        w = slice(col, col + P)
                        passes = [(st1_hi[:, w], c1_hi[:, s0:s1]), (st1_hi[:, w], c1_lo[:, s0:s1]),
                                  (st1_lo[:, w], c1_hi[:, s0:s1]), (st2[:, w], c2_hh[:, s0:s1]),
                                  (st2[0:R, w], c2_lo[:, s0:s1])]
                        for n, (a, b) in enumerate(passes):
                            mm = pe.matmul(o, a, b, start=(n == 0), stop=(n == len(passes) - 1))
                        mm.then_inc(job_done, 1)

            def fuse_q(g, step_g):
                pe.wait_ge(ld_qw, UNF * (g + 1))
                o = open_job(step_g, "m")
                for n in range(4):
                    half, h = n // 2, n % 2
                    mm = pe.matmul(o[:, n * R:(n + 1) * R], qnT[h][:, half * P:(half + 1) * P], wuk[h],
                                   start=(n == 0), stop=(n == 3), skip_group_check=True)
                mm.then_inc(job_done, 1)

            def score_row(g, h, j):
                bank = open_use(g, f"row{h}{j}").bank
                chunks = 2 if ROW_W[j] > BANK else 1
                w = ROW_W[j] // chunks
                for c in range(chunks):
                    o = bank_ps[:, bank + c, 0:w]
                    q0 = P * j + c * w
                    kk = slice(P * j, P * j + P)
                    pe.matmul(o, key_hi[:, h, kk], q_hi[:, h, q0:q0 + w], start=True, stop=False)
                    pe.matmul(o, key_hi[:, h, kk], q_lo[:, h, q0:q0 + w], start=False, stop=False)
                    if c == 0:
                        pe.matmul(o[:, 0:P], id16[:, :], causal16[:, :], start=False, stop=False)
                    mm = pe.matmul(o, key_lo[:, h, kk], q_hi[:, h, q0:q0 + w], start=False, stop=True)
                mm.then_inc(row_done, 1)

            def turn(g, kind, h, src):
                v = src.rearrange("p (q i) -> p i q", i=T)
                for c in range(2):
                    o = open_job(g, f"{kind}{'ab'[h]}_{c}")
                    for i in range(4):
                        mm = pe.transpose(o[:, P * i:P * i + P], v[:, 4 * c + i, :], id32[:, :])
                    mm.then_inc(job_done, 1)

            def step(g, par):
                scores, queries_, vals, output = parts(g)
                if scores:
                    pe.wait_ge(qk_hi_set, 4 * (g + 2))
                    pe.wait_ge(qk_lo_set, 4 * (g + 2))
                    for h in range(2):
                        for j in range(T):
                            score_row(g, h, j)
                if queries_:
                    fuse_q(g + 1, g)
                if vals:
                    pe.wait_ge(summed, (2 * g - 1) * T)
                    turn(g, "l", 0, psum_p[:, 0, :])

                def outputs(lo, hi):
                    for i in range(lo, hi):
                        o = open_job(g, f"o_{i}")
                        a, b = att_hi[:, i * P:(i + 1) * P], att_lo[:, i * P:(i + 1) * P]
                        pe.matmul(o, a, n_hi[:, :], start=True, stop=False)
                        pe.matmul(o, a, n_lo[:, :], start=False, stop=False)
                        pe.matmul(o, b, n_hi[:, :], start=False, stop=True).then_inc(job_done, 1)

                if output:
                    pe.wait_ge(att_hi_set, g - 1)
                    pe.wait_ge(att_lo_set, g - 1)
                    pe.wait_ge(n_hi_set, g - 1)
                    pe.wait_ge(dve_read, Use(g, "n", back=1).read)
                    outputs(0, 4)
                if scores:
                    pe.wait_ge(row_maxed, (2 * g + 1) * T)
                    turn(g, "t", 0, top[:, 0, :])
                    pe.wait_ge(row_maxed, (2 * g + 2) * T)
                    turn(g, "t", 1, top[:, 1, :])
                if queries_:
                    queries(g + 1, g, (0,))
                if output:
                    outputs(4, 8)
                if queries_:
                    queries(g + 1, g, (1,))
                if vals:
                    pe.wait_ge(ld_ow, UNF * g)
                    o = open_job(g, "n")
                    for h in range(2):
                        mm = pe.matmul(o[R * h:R * h + R, :], wuv[h], wout[h], start=True, stop=True)
                    mm.then_inc(job_done, 1)
                    if output:
                        pe.wait_ge(att_scaled, g - 1)
                    slot = 2 * (1 - par)
                    for j in range(T):
                        if j == LB_AFTER:
                            pe.wait_ge(summed, 2 * g * T)
                            turn(g, "l", 1, psum_p[:, 1, :])
                        pe.wait_ge(exped, (2 * g - 1) * len(CHUNKS) + CHUNK_OF[j] + 1)
                        for c in range(2):
                            s0, s1 = max(c * BANK, P * j), (c + 1) * BANK
                            if s0 >= s1:
                                continue
                            for h in range(2):
                                mm = pe.matmul(att_ps[R * h:R * h + R, c, s0 - c * BANK:], values[:, j, :],
                                               row(slot + h, j)[:, s0 - P * j:s1 - P * j],
                                               start=(j == 0), stop=(j == 4 * c + 3))
                    mm.then_inc(att_done, 1)

            pe.wait_ge(ld_cq, 5 * UNF)
            for part in range(2):
                for c in range(2):
                    o = open_job(None, f"cq{part + 1}_{c}")
                    for k in range(KD):
                        mm = pe.matmul(o, wqd_sb[:, k, part * P:(part + 1) * P], xT_sb[:, k, c * BANK:(c + 1) * BANK],
                                       start=(k == 0), stop=(k == KD - 1))
                    mm.then_inc(job_done, 1)
            pe.wait_ge(ld_k, UNF)
            for c in range(2):
                for n, name in enumerate("zab"):
                    o = open_job(None, f"k{name}_{c}")
                    for k in range(KD):
                        mm = pe.matmul(o, wk_sb[:, k, n * P:(n + 1) * P], xT_sb[:, k, c * BANK:(c + 1) * BANK],
                                       start=(k == 0), stop=(k == KD - 1))
                    mm.then_inc(job_done, 1)
            for c in range(2):
                o = open_job(None, f"v_{c}")
                for i in range(4):
                    t = 4 * c + i
                    for k in range(KD):
                        mm = pe.matmul(o[:, i * R:(i + 1) * R], xT_sb[:, k, t * P:(t + 1) * P], wk_sb[:, k, P:P + R],
                                       start=(k == 0), stop=(k == KD - 1))
                mm.then_inc(job_done, 1)
            fuse_q(0, None)
            pe.wait_ge(c_hi_set, 4)
            pe.wait_ge(dve_read, Use(None, "cq2_1").read)
            queries(0, None, (0, 1))
            pe.wait_ge(ld_id, 3 * UNF)
            pe.wait_ge(act_read, Use(None, "v_1").read)
            run_steps(pe, step)

            rows = [bank_ps[:, n, :] for n in range(4)]
            jobs = [bank_ps[:, n, :] for n in (4, 5)]
            pe.wait_ge(dve_read, ALL_READS["dve"])
            for i in range(T):
                pe.wait_ge(x1_set, i + 1)
                if i >= 2:
                    pe.wait_ge(x1T_set, i - 1)
                for k in range(KD):
                    mm = pe.transpose(jobs[i % 2][:, k * P:(k + 1) * P], y[:, i, k * P:(k + 1) * P], id32[:, :])
                mm.then_inc(x1_turned, 1)
            pe.wait_ge(ld_ffn, 3 * UNF)
            for i in range(T):
                pe.wait_ge(x1T_set, i + 1)
                if i >= 4:
                    pe.wait_ge(hr_set, i - 3)
                for k in range(KD):
                    mm = pe.matmul(rows[i % 4][:, 0:HW], x1T[:, k, i * P:(i + 1) * P], hr_w[:, k, :],
                                   start=(k == 0), stop=(k == KD - 1))
                mm.then_inc(hr_done, 1)

            ff_banks = ffn_banks(rows, jobs)

            def base(i):
                for k in range(KD):
                    pe.matmul(ff_banks[i], x1T[:, k, i * P:(i + 1) * P], base_w[:, k, :], start=(k == 0), stop=False)

            def lora_up(i):
                pe.matmul(ff_banks[i], hT[:, i * P:(i + 1) * P], up_w, start=False, stop=True).then_inc(ff_done, 1)

            for i in range(4):
                base(i)
            pe.wait_ge(hr_set, T)
            for i in range(4, 6):
                base(i)
            pe.wait_ge(hw_set, 1)
            for c in range(2):
                for i in range(4):
                    mm = pe.transpose(rows[2 + c][:, i * P:(i + 1) * P], hw[:, 4 * c + i, :], id32[:, :])
                mm.then_inc(hw_turned, 1)
            pe.wait_ge(hT_set, 2)
            for i in range(6):
                lora_up(i)
            for i in range(6, T):
                base(i)
                lora_up(i)

        @block.scalar
        def _(act):
            def job(g, name):
                use = Use(g, name)
                act.wait_ge(job_done, use.done)
                return bank_ps[:, use.bank, :]

            def rotary_weights(g):
                act.wait_ge(ld_qw, UNF * (g + 1))
                for st, raw in ((st1_hi, wr1), (st2, wr2)):
                    act.activation(rot_cols(st[:, :]), raw.rearrange("p (a b) -> p a b", a=2), ACT.Copy
                                   ).then_inc(st_rot_hi, 1)

            def latent_weights(step_g):
                o = job(step_g, "m")
                for n, st in enumerate((st1_hi, st2)):
                    act.activation(lat_cols(st[:, :]), o[:, n * P:(n + 1) * P].rearrange("p (a b) -> p a b", a=2),
                                   ACT.Copy).then_inc(st_lat_hi, 1)

            def queries(n, step_g, kind, hi):
                for c in range(2):
                    for h in range(2):
                        o = job(step_g, f"{kind}{'ab'[h]}_{c}")
                        lat = slice(R * h, R * h + R)
                        if c > 0 or not isinstance(n, int) or n > 0:
                            act.wait_ge(qk_lo_set, 4 * n + 2 * c + h - 1)
                        act.wait_ge(rot_set, 4 * n + 2 * c + h + 1)
                        act.activation(fused[lat, h, :], o[lat, :], ACT.Copy).then_inc(act_read, 1)
                    for h in range(2):
                        act.wait_ge(fused_set, 4 * n + 2 * c + h + 1)
                        act.wait_ge(act_read, Use(step_g, f"{kind}{'ab'[h]}_{c}").read)
                        act.activation(hi[:, h, c * BANK:(c + 1) * BANK], fused[:, h, :], ACT.Copy
                                       ).then_inc(qk_hi_set, 1)

            def exp_chunk(head, slot, c):
                js = CHUNKS[c]
                act.wait_ge(centred, head * T + js[-1] + 1)
                part = ring[:, slot, ROW_AT[js[0]]:ROW_AT[js[-1]] + ROW_W[js[-1]]]
                act.activation(part, part, ACT.Exp, scale=SCALE).then_inc(exped, 1)

            def copy_row(g, h, j, slot):
                use = Use(g, f"row{h}{j}")
                act.wait_ge(row_done, use.done)
                w = ROW_W[j]
                if w > BANK:
                    src = bank_ps[:, use.bank:use.bank + 2, 0:w // 2]
                    dst = row(slot, j).rearrange("p (c w) -> p c w", c=2)
                else:
                    src, dst = bank_ps[:, use.bank, 0:w], row(slot, j)
                act.activation(dst, src, ACT.Copy).then_inc(row_copied, 1)

            def step(g, par):
                scores, queries_, vals, output = parts(g)
                a_slot, old_b = 2 * par, 2 * (1 - par) + 1
                if output:
                    act.wait_ge(att_done, g - 1)
                    act.wait_ge(summed, (2 * g - 2) * T)
                for h in range(2):
                    for j in range(T):
                        if scores:
                            copy_row(g, h, j, 2 * par + h)
                        if output and (h, j) == (1, 0):
                            act.wait_ge(att_scaled, g - 1)
                            act.activation(att_hi[:, :], att[:, :], ACT.Copy).then_inc(att_hi_set, 1)
                        if queries_ and (h, j) == (1, 3):
                            rotary_weights(g + 1)
                        if vals and (h, j) in EXP_B:
                            exp_chunk(2 * g - 1, old_b, EXP_B[h, j])
                if queries_:
                    latent_weights(g)
                    queries(g + 2, g, "f", q_hi)
                if vals:
                    act.activation(n_hi[:, :], job(g, "n"), ACT.Copy).then_inc(n_hi_set, 1)
                if scores:
                    for c in range(len(CHUNKS)):
                        exp_chunk(2 * g, a_slot, c)

            for part, hi in enumerate((c1_hi, c2_hh)):
                for c in range(2):
                    o = job(None, f"cq{part + 1}_{c}")
                    act.activation(hi[:, c * BANK:(c + 1) * BANK], o, ACT.Copy).then_inc(c_hi_set, 1)
            rotary_weights(0)
            queries(0, None, "k", key_hi)
            for c in range(2):
                o = job(None, f"v_{c}")
                act.activation(values[:, 4 * c:4 * c + 4, :], o[:, 0:4 * R].rearrange("p (i r) -> p i r", i=4), ACT.Copy
                               ).then_inc(act_read, 1)
            latent_weights(None)
            queries(1, None, "f", q_hi)
            run_steps(act, step)

            act.wait_ge(mean_linked, 2 * T + 1)
            act.activation(thin[0], moments[:, :, 1], ACT.Sqrt, bias=eps_sb).then_inc(spread_ready, 1)
            for i in range(T):
                act.wait_ge(x1_turned, i + 1)
                act.activation(x1T[:, :, i * P:(i + 1) * P], bank_ps[:, 4 + i % 2, :].rearrange("p (k s) -> p k s", k=KD),
                               ACT.Copy).then_inc(x1T_set, 1)
            act.wait_ge(logits_centred, 1)
            act.activation(small[1], small[0], ACT.Exp).then_inc(logits_exped, 1)
            for c in range(2):
                act.wait_ge(hw_turned, c + 1)
                act.activation(hT[:, c * BANK:(c + 1) * BANK], bank_ps[:, 2 + c, :], ACT.Copy
                               ).then_inc(hT_set, 1)
            for i in range(T):
                act.wait_ge(var_ready, i + 1)
                act.activation(thin[8][:, i:i + 1], moments[:, i, 1:2], ACT.Sqrt, bias=eps_sb).then_inc(sd_ready, 1)

        @block.gpsimd
        def _(pool):
            def rotary_weights(g):
                pool.wait_ge(st_rot_hi, 2 * g + 1)
                if isinstance(g, int) and g == 0:
                    pool.wait_ge(ld_qw, UNF)
                pool.tensor_tensor(rot_cols(st1_lo[:, :]), wr1.rearrange("p (a b) -> p a b", a=2),
                                   rot_cols(st1_hi[:, :].bitcast(F32)), ALU.subtract).then_inc(st_rot_lo, 1)
                pool.wait_ge(st_rot_hi, 2 * g + 2)
                pool.wait_ge(st_rot_lo, 2 * g + 1)
                low = slice(R, P)
                pool.tensor_tensor(rot_cols(st2[low, :]), wr2[low, :].rearrange("p (a b) -> p a b", a=2),
                                   rot_cols(st2[low, :].bitcast(F32)), ALU.subtract).then_inc(st_rot_lo, 1)
                pool.wait_ge(st_rot_lo, 2 * g + 2)

            def queries(n, hi, lo):
                for c in range(2):
                    for h in range(2):
                        if h == 1:
                            pool.wait_ge(fused_set, 4 * n + 2 * c + 1)
                        elif c == 1 or not isinstance(n, int) or n > 0:
                            pool.wait_ge(qk_lo_set, 4 * n + 2 * c)
                        pool.wait_ge(rot_set, 4 * n + 2 * c + h + 1)
                        rot = slice(R * (1 - h), R * (1 - h) + R)
                        pool.tensor_tensor(fused[rot, h, :], fused[rot, h, :], turned[rot, :], ALU.add
                                           ).then_inc(fused_set, 1)
                    pool.wait_ge(fused_set, 4 * n + 2 * c + 2)
                    for h in range(2):
                        pool.wait_ge(qk_hi_set, 4 * n + 2 * c + h + 1)
                        cols = slice(c * BANK, (c + 1) * BANK)
                        pool.tensor_tensor(lo[:, h, cols], fused[:, h, :], hi[:, h, cols].bitcast(F32), ALU.subtract
                                           ).then_inc(qk_lo_set, 1)

            def sum_head(head, h, slot, prev):
                acc = psum_p[:, h, :]
                if prev is not None:
                    pool.wait_ge(job_done, prev)
                for j in range(1, T):
                    pool.wait_ge(exped, head * len(CHUNKS) + CHUNK_OF[j] + 1)
                    if j > 1:
                        pool.wait_ge(summed, head * T + j)
                    before = row(slot, 0)[:, P:] if j == 1 else acc[:, P * j:]
                    pool.tensor_tensor(acc[:, P * j:], before, row(slot, j), ALU.add).then_inc(summed, 1)
                    if j == 1:
                        pool.tensor_copy(acc[:, 0:P], row(slot, 0)[:, 0:P]).then_inc(summed, 1)

            def step(g, par):
                scores, queries_, vals, output = parts(g)
                if output:
                    pool.wait_ge(att_hi_set, g - 1)
                    pool.tensor_tensor(att_lo[:, :], att[:, :], att_hi[:, :].bitcast(F32), ALU.subtract
                                       ).then_inc(att_lo_set, 1)
                if queries_:
                    rotary_weights(g + 1)
                if vals:
                    sum_head(2 * g - 1, 1, 2 * (1 - par) + 1, Use(g, "lb_1", back=1).done if output else None)
                    pool.wait_ge(summed, 2 * g * T)
                if queries_:
                    queries(g + 2, q_hi, q_lo)
                if scores:
                    sum_head(2 * g, 0, 2 * par, Use(g, "la_1").done if vals else None)

            rotary_weights(0)
            queries(0, key_hi, key_lo)
            queries(1, q_hi, q_lo)
            run_steps(pool, step)

            pool.wait_ge(ld_ffn, 3 * UNF)
            for i in range(T):
                pool.wait_ge(x1_set, i + 1)
                pool.tensor_tensor(res[:, i, :], y[:, i, :], bias_sb, ALU.add).then_inc(x1b_set, 1)

        @block.vector
        def _(dve):
            def job(g, name):
                use = Use(g, name)
                dve.wait_ge(job_done, use.done)
                return bank_ps[:, use.bank, :]

            def latent_weights(n, step_g):
                o = job(step_g, "m")
                dve.wait_ge(st_lat_hi, 2 * n + 2)
                low = slice(R, P)
                dve.tensor_tensor(lat_cols(st2[low, :]), o[low, P:2 * P].rearrange("p (a b) -> p a b", a=2),
                                  lat_cols(st2[low, :].bitcast(F32)), ALU.subtract).then_inc(st_lat_lo, 1)
                dve.tensor_tensor(lat_cols(st1_lo[:, :]), o[:, 0:P].rearrange("p (a b) -> p a b", a=2),
                                  lat_cols(st1_hi[:, :].bitcast(F32)), ALU.subtract).then_inc(dve_read, 1)

            def queries(n, step_g, kind, chunks=(0, 1)):
                for c in chunks:
                    cols = slice(c * BANK, (c + 1) * BANK)
                    o = job(step_g, f"{kind}z_{c}")
                    if c > 0 or not isinstance(n, int) or n > 0:
                        dve.wait_ge(fused_set, 4 * n + 2 * c)
                    dve.tensor_tensor(turned[:, :], o, cos_sin[:, 1, cols], ALU.mult).then_inc(dve_read, 1)
                    for h in range(2):
                        rot = slice(R * (1 - h), R * (1 - h) + R)
                        o = job(step_g, f"{kind}{'ab'[h]}_{c}")
                        if c > 0 or not isinstance(n, int) or n > 0:
                            dve.wait_ge(qk_lo_set, 4 * n + 2 * c + h - 1)
                        dve.tensor_tensor(fused[rot, h, :], o[rot, :], cos_sin[rot, 0, cols], ALU.mult
                                          ).then_inc(rot_set, 1)

            def max_row(g, h, j, slot):
                n = (2 * g + h) * T + j
                acc = top[:, h, :]
                dve.wait_ge(row_copied, n + 1)
                if j == 0:
                    dve.tensor_copy(acc[:, 0:P], row(slot, 0)[:, 0:P]).then_inc(row_maxed, 1)
                    return
                if j > 1:
                    dve.wait_ge(row_maxed, n)
                before = row(slot, 0)[:, P:] if j == 1 else acc[:, P * j:]
                dve.tensor_tensor(acc[:, P * j:], before, row(slot, j), ALU.max).then_inc(row_maxed, 1)

            def centre_row(head, h, j, slot):
                if j == 0:
                    dve.wait_ge(max_loaded[h], (head + 2 - h) * (UNF // 2))
                    dve.wait_ge(row_copied, (head + 1) * T)
                r = row(slot, j)
                dve.tensor_tensor(r, r, maxes[:, h, P * j:], ALU.subtract).then_inc(centred, 1)

            def reduce_turned(g, kind, h, col, op):
                for c in range(2):
                    o = job(g, f"{kind}{'ab'[h]}_{c}")
                    dve.tensor_reduce(col[:, h, 4 * c:4 * c + 4], o.rearrange("p (i t) -> p i t", i=4), AX_X, op
                                      ).then_inc(dve_read, 1)

            def invert(g, h):
                dve.wait_ge(dve_read, Use(g, f"l{'ab'[h]}_1").read)
                dve.reciprocal(inv_col[:, h, :], sum_col[:, h, :]).then_inc(inv_ready, 1)

            def add_output(g, lo, hi):
                for i in range(lo, hi):
                    o = job(g, f"o_{i}")
                    dve.tensor_tensor(y[:, i, :], y[:, i, :], o, ALU.add).then_inc(dve_read, 1)

            def step(g, par):
                scores, queries_, vals, output = parts(g)
                a_slot, b_slot, old_b = 2 * par, 2 * par + 1, 2 * (1 - par) + 1
                for j in range(T):
                    if scores:
                        max_row(g, 0, j, a_slot)
                    if vals and j > 0 and EARLY_ROWS + j - 1 < T:
                        centre_row(2 * g - 1, 1, EARLY_ROWS + j - 1, old_b)
                    if output and j == 3:
                        dve.wait_ge(att_done, g - 1)
                        dve.wait_ge(inv_loaded, (g - 1) * 2 * UNF)
                        dve.tensor_tensor(att[:, :], att[:, :], att_ps[:, :, :].rearrange("p c n -> p (c n)"), ALU.mult
                                          ).then_inc(att_scaled, 1)
                if scores:
                    for j in range(T):
                        max_row(g, 1, j, b_slot)
                if queries_:
                    latent_weights(g + 1, g)
                if vals:
                    reduce_turned(g, "l", 0, sum_col, ALU.add)
                    invert(g, 0)
                if output:
                    add_output(g, 0, 4)
                if scores:
                    reduce_turned(g, "t", 0, max_col, ALU.max)
                    reduce_turned(g, "t", 1, max_col, ALU.max)
                if queries_:
                    queries(g + 2, g, "f", (0,))
                if output:
                    add_output(g, 4, 8)
                if queries_:
                    queries(g + 2, g, "f", (1,))
                if scores:
                    for j in range(3):
                        centre_row(2 * g, 0, j, a_slot)
                if vals:
                    o = job(g, "n")
                    dve.wait_ge(n_hi_set, g)
                    dve.tensor_tensor(n_lo[:, :], o, n_hi[:, :].bitcast(F32), ALU.subtract).then_inc(dve_read, 1)
                    reduce_turned(g, "l", 1, sum_col, ALU.add)
                    invert(g, 1)
                if scores:
                    for j in range(3, T):
                        centre_row(2 * g, 0, j, a_slot)
                    for j in range(EARLY_ROWS):
                        centre_row(2 * g + 1, 1, j, b_slot)

            n = 0
            for part, (hi, lo) in enumerate(((c1_hi, c1_lo), (c2_hh, c2_lo))):
                for c in range(2):
                    o = job(None, f"cq{part + 1}_{c}")
                    n += 1
                    dve.wait_ge(c_hi_set, n)
                    rows = slice(0, P if part == 0 else R)
                    cols = slice(c * BANK, (c + 1) * BANK)
                    dve.tensor_tensor(lo[rows, cols], o[rows, :], hi[rows, cols].bitcast(F32), ALU.subtract
                                      ).then_inc(dve_read, 1)
            dve.wait_ge(ld_tab, UNF)
            queries(0, None, "k")
            latent_weights(0, None)
            queries(1, None, "f")
            dve.wait_ge(ld_y, UNF)
            run_steps(dve, step)

            linked = [0]

            def link(ins):
                linked[0] += 1
                ins.then_inc(mean_linked, 1)
                dve.wait_ge(mean_linked, linked[0])

            dve.wait_ge(dve_read, ALL_READS["dve"])
            link(dve.memset(eps_sb, EPS))
            for i in range(T):
                link(dve.bn_stats(stats[:, i, :], y[:, i, :]))
            for i in range(T):
                link(dve.bn_aggr(moments[:, i, :], stats[:, i, :]))
            dve.wait_ge(spread_ready, 1)
            link(dve.reciprocal(thin[1], thin[0]))
            for i in range(T):
                dve.tensor_scalar(y[:, i, :], y[:, i, :], moments[:, i, 0:1], thin[1][:, i:i + 1], ALU.subtract, ALU.mult
                                  ).then_inc(x1_set, 1)
            for i in range(T):
                dve.wait_ge(hr_done, i + 1)
                dve.tensor_copy(hr[:, i, :], bank_ps[:, i % 4, 0:HW]).then_inc(hr_set, 1)
            dve.wait_ge(hr_set, T)

            def over(t):
                return t.unsqueeze(2).broadcast_to([P, T, NE])

            logits = hr[:, :, NE * RANK:]
            centred_l, probs, is_top, ranked, first, rest, second, weight = small
            top1, total, inv_total, at1, top2, at2 = thin[2:8]
            link(dve.tensor_reduce(top1, logits, AX_X, ALU.max))
            dve.tensor_tensor(centred_l, logits, over(top1), ALU.subtract).then_inc(logits_centred, 1)
            dve.wait_ge(logits_exped, 1)
            link(dve.tensor_reduce(total, probs, AX_X, ALU.add))
            link(dve.reciprocal(inv_total, total))
            link(dve.tensor_tensor(probs, probs, over(inv_total), ALU.mult))

            dve.wait_ge(ld_ffn, 3 * UNF)

            def take_largest(values_, largest, place, chosen):
                link(dve.tensor_reduce(largest, values_, AX_X, ALU.max))
                link(dve.tensor_tensor(is_top, values_, over(largest), ALU.is_equal))
                link(dve.tensor_tensor(ranked, is_top, rank_sb, ALU.mult))
                link(dve.tensor_reduce(place, ranked, AX_X, ALU.max))
                link(dve.tensor_tensor(chosen, rank_sb, over(place), ALU.is_equal))

            take_largest(probs, top1, at1, first)
            link(dve.scalar_tensor_tensor(out=rest, in0=first, scalar=-2.0, in1=probs, op0=ALU.mult, op1=ALU.add))
            take_largest(rest, top2, at2, second)
            link(dve.tensor_tensor(weight, first, second, ALU.add))
            link(dve.tensor_tensor(weight, weight, probs, ALU.mult))
            link(dve.tensor_tensor(total, top1, top2, ALU.add))
            link(dve.reciprocal(inv_total, total))
            link(dve.scalar_tensor_tensor(out=weight, in0=weight, scalar=LORA_SCALE, in1=over(inv_total),
                                          op0=ALU.mult, op1=ALU.mult))
            for i in range(T):
                ins = dve.tensor_tensor(hw[:, i, :].rearrange("p (e r) -> p e r", e=NE),
                                        hr[:, i, 0:NE * RANK].rearrange("p (e r) -> p e r", e=NE),
                                        weight[:, i, :].unsqueeze(2).broadcast_to([P, NE, RANK]), ALU.mult)
            ins.then_inc(hw_set, 1)

            ff_banks = ffn_banks([bank_ps[:, n, :] for n in range(4)], [bank_ps[:, n, :] for n in (4, 5)])

            def finish(i):
                dve.wait_ge(sd_ready, i + 1)
                link(dve.reciprocal(thin[9][:, i:i + 1], thin[8][:, i:i + 1]))
                dve.tensor_scalar(res[:, i, :], res[:, i, :], moments[:, i, 0:1], thin[9][:, i:i + 1],
                                  ALU.subtract, ALU.mult).then_inc(res_set, 1)

            for i in range(T):
                dve.wait_ge(x1b_set, i + 1)
                dve.wait_ge(ff_done, i + 1)
                link(dve.tensor_tensor(res[:, i, :], res[:, i, :], ff_banks[i], ALU.add))
                link(dve.bn_stats(stats[:, i, :], res[:, i, :]))
                dve.bn_aggr(moments[:, i, :], stats[:, i, :]).then_inc(var_ready, 1)
                if i > 0:
                    finish(i - 1)
            finish(T - 1)


def kernel(**inputs):
    import numpy as np
    import concourse.bacc as bacc
    from concourse import mybir as mb
    from concourse.bass_utils import run_bass_kernel_spmd

    def get(name):
        return np.asarray(inputs[name])

    def tiles(a):
        return np.ascontiguousarray(a.reshape(-1, 128, a.shape[-1]).transpose(1, 0, 2))

    def swap(a):
        return np.concatenate([a[..., 32:], a[..., :32]], -1)

    x = get("L0_attn_hidden_states")[0]
    w_qd = get("L0_attn_w_q_down")
    w_kv, w_kr = get("L0_attn_w_kv_down"), get("L0_attn_w_k_rope")
    nope = get("L0_attn_w_q_up_nope").reshape(192, 32, 128).transpose(1, 2, 0)
    nope = np.concatenate([nope, nope[:, :, 128:]], -1)
    nope = nope.reshape(16, 2, 128, 256).transpose(0, 2, 1, 3).reshape(16, 128, 512)
    uk = get("L0_attn_w_uk").reshape(16, 2, 128, 64).transpose(0, 2, 1, 3).reshape(16, 128, 128)
    rope = get("L0_attn_w_q_up_rope").reshape(192, 16, 2, 64).transpose(1, 0, 2, 3)
    rot = np.concatenate([swap(rope[:, :, 1]), swap(rope[:, :, 0]), rope[:, :, 0], rope[:, :, 1]], -1)
    qw = np.concatenate([nope, uk, rot[:, 0:128], np.concatenate([rot[:, 128:], rot[:, 128:]], 1)], -1)
    uv = get("L0_attn_w_uv").reshape(16, 2, 128, 64).transpose(0, 2, 1, 3).reshape(16, 128, 128)
    wo = get("L0_attn_w_out").reshape(16, 2, 128, 512).transpose(0, 2, 1, 3).reshape(16, 128, 1024)

    f32 = np.float32
    freqs = f32(1.0) / f32(10000.0) ** (np.arange(0, 64, 2, dtype=f32) / f32(64))
    ramp = np.clip((f32(2.0 * np.pi) / freqs / f32(4096.0) - f32(1.0)) / f32(31.0), f32(0), f32(1))
    inv_freq = freqs / (f32(1.0) - ramp + ramp * f32(40.0))
    angle = (np.arange(1024, dtype=f32)[:, None] * inv_freq[None, :]).T
    cos, sin = np.cos(angle), np.sin(angle)
    tables = np.stack([np.tile(cos, (4, 1)), np.concatenate([-sin, sin, -sin, sin], 0)], 1).astype(f32)

    import ml_dtypes
    t = np.arange(128)
    arrays = {
        "in_xT": np.ascontiguousarray(tiles(np.ascontiguousarray(x.T))),
        "in_x": x,
        "in_wq_down": tiles(np.concatenate([w_qd, w_qd[:, 128:]], -1)),
        "in_wk": tiles(np.concatenate([swap(w_kr), swap(w_kr), w_kv, w_kr, w_kr, w_kv], -1)),
        "in_qw": qw, "in_ow": np.concatenate([uv, wo], -1),
        "in_tables": tables,
        "in_ident": np.eye(128, dtype=f32),
        "in_ident16": np.eye(128, dtype=f32).astype(ml_dtypes.bfloat16),
        "in_mask16": np.where(t[None, :] < t[:, None], f32(-3e38), f32(0)).astype(ml_dtypes.bfloat16),
        "in_rank": np.tile(np.arange(8, 0, -1).astype(f32), (128, 8)),
        "in_ffn": np.concatenate([
            tiles(get("L0_ffn_W_base").T).reshape(128, -1),
            tiles(np.concatenate([get("L0_ffn_A").reshape(128, 512).T, get("L0_ffn_W_router").T], -1)).reshape(128, -1),
            get("L0_ffn_B").transpose(0, 2, 1).reshape(128, 512)], -1),
        "in_bias": get("L0_ffn_b_base")[None, :],
    }
    arrays = {k: np.ascontiguousarray(v) for k, v in arrays.items()}
    nc = bacc.Bacc("TRN2", target_bir_lowering=False, num_devices=1)
    args = [nc.dram_tensor(k, v.shape, mb.dt.from_np(v.dtype), kind="ExternalInput").ap() for k, v in arrays.items()]
    out = nc.dram_tensor("out", (1024, 512), mb.dt.float32, kind="ExternalOutput").ap()
    build(nc, *args, out)
    r = run_bass_kernel_spmd(nc, [arrays], core_ids=[0])
    return r.results[0]["out"].reshape(1, 1024, 512)
```

```python
from contextlib import ExitStack

import concourse.bass as bass
from concourse import mybir

F32 = mybir.dt.float32
F32R = mybir.dt.float32r
BF16 = mybir.dt.bfloat16
ALU = mybir.AluOpType
ACT = mybir.ActivationFunctionType
AX_X = mybir.AxisListType.X

P = 128
S = 1024
D = 512
H = 32
QL = 192
R = 64
DN = 128
PAIRS = H // 2
T = S // P
KD = D // P
BANK = 512
NE, RANK = 8, 16
LORA_SCALE = 32 / RANK
EPS = 1e-5
SCALE = float(1.0 / (DN + R) ** 0.5)

ROW_W = [S - P * j for j in range(T)]
ROW_AT = [sum(ROW_W[:j]) for j in range(T)]
HEAD_COLS = sum(ROW_W)
CHUNKS = [(0,), (1, 2), (3, 4), (5, 6, 7)]
EARLY_ROWS = 5
EXP_B = {(0, 3): 0, (0, 7): 1, (1, 4): 2, (1, 7): 3}
CHUNK_OF = [c for j in range(T) for c in range(len(CHUNKS)) if j in CHUNKS[c]]

Z_AT, A_AT, B_AT, ST_W = 0, 128, 256, 384
UNF = 16

BANKS = 6
PRE = [f"cq{part}_{c}" for part in (1, 2) for c in range(2)] + ["m", "ka_0", "kb_1", "kz"] \
    + [f"f{n}_{c}" for c in range(2) for n in "zab"] + ["v_0"]


def step_uses(g):
    s, f, p, o = g < PAIRS, g + 1 < PAIRS, 1 <= g <= PAIRS, g >= 2
    first, second = [f"o_{i}" for i in range(4)], [f"o_{i}" for i in range(4, 8)]
    if not s:
        return ["la_0", "la_1", "lb_0", "lb_1", *first, *second, "n"] if p else first + second
    turns = ["ta_0", "ta_1", "tb_0", "tb_1"]
    uses = [f"row{h}{j}" for h in range(2) for j in range(T)]
    if not f:
        return uses + ["la_0", "la_1", *turns, *first, *second, "n", "lb_0", "lb_1"]
    uses += ["m"]
    if p:
        uses += ["la_0", "la_1"]
    if o:
        uses += first
    uses += turns + [f"f{n}_0" for n in "zab"]
    if o:
        uses += second
    uses += [f"f{n}_1" for n in "zab"]
    if g == 0:
        uses += ["v_1"]
    if p:
        uses += ["n", "lb_0", "lb_1"]
    return uses


def reader(name):
    if name.startswith("row"):
        return "row"
    return "act" if name[:2] in ("ka", "kb", "fa", "fb", "v_") else "dve"


STEPS = PAIRS + 2
STEADY = 2
LOOP = (STEADY + 1, PAIRS - 3)


def plan():
    written, reads = {"row": 0, "job": 0}, {"row": 0, "act": 0, "dve": 0}
    holds = [None] * BANKS
    table = {}
    for g in [None, *range(STEPS)]:
        bank = 0
        for name in PRE if g is None else step_uses(g):
            wide = name.startswith("row") and ROW_W[int(name[-1])] > BANK
            if wide and bank % 2:
                bank += 1
            banks = [bank % BANKS] + [bank % BANKS + 1] * wide
            bank += 1 + wide
            who = reader(name)
            kind = "row" if who == "row" else "job"
            written[kind] += 1
            reads[who] += 1
            before = sorted({holds[b] for b in banks if holds[b]}, key=str)
            table[g, name] = (banks, written[kind], reads[who], before)
            for b in banks:
                holds[b] = (who, g, name)
    return table


PLAN = plan()
GROWTH = {who: sum(reader(u) == who for u in step_uses(STEADY)) for who in ("row", "act", "dve")}
GROWTH["job"] = GROWTH["act"] + GROWTH["dve"]


class Use:

    def __init__(self, g, name, back=0):
        self.fixed = g is None or isinstance(g, int)
        self.step, self.name = g, name
        at = g if g is None else g - back if self.fixed else STEADY
        banks, done, read, self.before = PLAN[at, name]
        self.bank = banks[0]
        who = reader(name)
        kind = "row" if who == "row" else "job"
        self.done = done if self.fixed else (g - (STEADY + back)) * GROWTH[kind] + done
        self.read = read if self.fixed else (g - (STEADY + back)) * GROWTH[who] + read

    def frees(self):
        if self.fixed:
            return [(who, Use(g, name).read) for who, g, name in self.before]
        return [(who, Use(self.step, name, back=STEADY + 1 - g).read)
                for who, g, name in PLAN[STEADY + 1, self.name][3]]


def build(nc, xT, xres, wq_down, wk, qw, ow, tables, ident, ident16, mask16, rank_tab, ffn_w, bias, out):
    with ExitStack() as ctx:
        def sb(name, shape, dt=F32):
            return ctx.enter_context(nc.sbuf_tensor(name, shape, dt))

        def ps(name, shape, dt=F32):
            return ctx.enter_context(nc.psum_tensor(name, shape, dt))

        def sem(name):
            return ctx.enter_context(nc.semaphore(name))

        ring = sb("ring", [P, 4, HEAD_COLS])
        key_hi = sb("key_hi", [P, 2, S], F32R)
        key_lo = sb("key_lo", [P, 2, S], F32R)
        q_hi = sb("q_hi", [P, 2, S], F32R)
        q_lo = sb("q_lo", [P, 2, S], F32R)
        turned = sb("turned", [P, BANK])
        fused = sb("fused", [P, 2, BANK])
        cos_sin = sb("cos_sin", [P, 2, S])
        c1_hi = sb("c1_hi", [P, S], F32R)
        c1_lo = sb("c1_lo", [P, S], F32R)
        c2_hh = sb("c2_hh", [P, S], F32R)
        c2_lo = sb("c2_lo", [P, S], F32R)
        top = sb("top", [P, 2, S])
        psum_p = sb("psum_p", [P, 2, S])
        maxes = sb("maxes", [P, 2, S])
        att = sb("att", [P, S])
        att_hi = sb("att_hi", [P, S], F32R)
        att_lo = sb("att_lo", [P, S], F32R)
        n_hi = sb("n_hi", [P, D], F32R)
        n_lo = sb("n_lo", [P, D], F32R)
        qw_sb = sb("qw_sb", [P, 2 * 256 + 2 * R + 512])
        ow_sb = sb("ow_sb", [P, 2 * R + 2 * D])
        st1_hi = sb("st1_hi", [P, ST_W], F32R)
        st1_lo = sb("st1_lo", [P, ST_W], F32R)
        st2 = sb("st2", [P, ST_W], F32R)
        y = sb("y", [P, T, D])
        values = sb("values", [P, T, R])
        id32 = sb("id32", [P, P])
        id16 = sb("id16", [P, P], BF16)
        causal16 = sb("causal16", [P, P], BF16)
        max_col = sb("max_col", [P, 2, T])
        sum_col = sb("sum_col", [P, 2, T])
        inv_col = sb("inv_col", [P, 2, T])

        bank_ps = ps("bank_ps", [P, BANKS, BANK])
        att_ps = ps("att_ps", [P, 2, BANK])

        max_dram = nc.dram_tensor("max_rows", (2, S), F32, kind="Internal").ap()
        inv_dram = nc.dram_tensor("inv_rows", (2, S), F32, kind="Internal").ap()

        def row(slot, j):
            return ring[:, slot, ROW_AT[j]:ROW_AT[j] + ROW_W[j]]

        flat = ring[:, :, :].rearrange("p a n -> p (a n)")
        at = [0]

        def carve(n):
            at[0] += n
            return flat[:, at[0] - n:at[0]]

        at[0] = 2 * HEAD_COLS
        xT_sb = carve(KD * S).rearrange("p (k s) -> p k s", k=KD)
        wqd_sb = carve(KD * 256).rearrange("p (k n) -> p k n", k=KD)
        wk_sb = carve(KD * 384).rearrange("p (k n) -> p k n", k=KD)
        assert at[0] <= 4 * HEAD_COLS
        at[0] = 0
        HW = NE * RANK + NE
        base_w = carve(KD * D).rearrange("p (k n) -> p k n", k=KD)
        hr_w = carve(KD * HW).rearrange("p (k n) -> p k n", k=KD)
        up_w = carve(D)
        bias_sb = carve(D)
        rank_sb = carve(T * NE).rearrange("p (i e) -> p i e", e=NE)
        x1T = carve(KD * S).rearrange("p (k s) -> p k s", k=KD)
        assert at[0] <= 2 * HEAD_COLS
        at[0] = 2 * HEAD_COLS
        hr = carve(T * HW).rearrange("p (i n) -> p i n", i=T)
        small = [carve(T * NE).rearrange("p (i e) -> p i e", e=NE) for _ in range(8)]
        thin = [carve(T) for _ in range(10)]
        stats = carve(T * 6).rearrange("p (i n) -> p i n", i=T)
        moments = carve(T * 2).rearrange("p (i n) -> p i n", i=T)
        eps_sb = carve(1)
        base_hi = key_hi[:, :, :].rearrange("p a s -> p (a s)").rearrange("p (k n) -> p k n", k=KD)
        base_lo = key_lo[:, :, :].rearrange("p a s -> p (a s)").rearrange("p (k n) -> p k n", k=KD)
        x1T_hi = [t[:, :, :].rearrange("p a s -> p (a s)")[:, i * D:(i + 1) * D].rearrange("p (k t) -> p k t", k=KD)
                  for t in (q_hi, q_lo) for i in range(T // 2)]
        x1T_lo = [t[:, i * D:(i + 1) * D].rearrange("p (k t) -> p k t", k=KD)
                  for t in (c1_hi, c1_lo, c2_hh, att_hi) for i in range(2)]
        up_hi, up_lo = n_hi[:, :], n_lo[:, :]
        hT_hi, hT_lo = att_lo[:, :], c2_lo[:, :]
        hw = carve(T * P).rearrange("p (i n) -> p i n", i=T)
        res = carve(T * D).rearrange("p (i n) -> p i n", i=T)
        assert at[0] <= 4 * HEAD_COLS

        qnT = [qw_sb[:, h * 256:(h + 1) * 256] for h in range(2)]
        wuk = [qw_sb[:, 512 + h * R:512 + (h + 1) * R] for h in range(2)]
        wr1 = qw_sb[:, 640:896]
        wr2 = qw_sb[:, 896:1152]
        wuv = [ow_sb[:, h * R:(h + 1) * R] for h in range(2)]
        wout = [ow_sb[:, 128 + h * D:128 + (h + 1) * D] for h in range(2)]

        def rot_cols(t):
            return t.rearrange("p (a b) -> p a b", b=192)[:, :, 0:128]

        def lat_cols(t):
            return t.rearrange("p (a b) -> p a b", b=192)[:, :, 128:192]

        ld_x = [sem(f"ld_x{k}") for k in range(KD)]
        keys_swapped = sem("keys_swapped")
        ld_k = sem("ld_k")
        ld_tab = sem("ld_tab")
        ld_id = sem("ld_id")
        ld_y = sem("ld_y")
        ld_qw = sem("ld_qw")
        ld_ow = sem("ld_ow")
        ld_base = sem("ld_base")
        ld_ffn = sem("ld_ffn")
        max_written = sem("max_written")
        max_loaded = [sem("max_loaded_a"), sem("max_loaded_b")]
        inv_written = sem("inv_written")
        inv_loaded = sem("inv_loaded")
        job_done = sem("job_done")
        dve_read = sem("dve_read")
        act_read = sem("act_read")
        row_done = sem("row_done")
        row_copied = sem("row_copied")
        row_maxed = sem("row_maxed")
        centred = sem("centred")
        exped = sem("exped")
        summed = sem("summed")
        inv_ready = sem("inv_ready")
        att_done = sem("att_done")
        first_half_done = sem("first_half_done")
        att_scaled = sem("att_scaled")
        att_hi_set = sem("att_hi_set")
        att_lo_set = sem("att_lo_set")
        n_hi_set = sem("n_hi_set")
        c_hi_set = sem("c_hi_set")
        rot_set = sem("rot_set")
        fused_set = sem("fused_set")
        qk_hi_set = sem("qk_hi_set")
        qk_lo_set = sem("qk_lo_set")
        st_rot_hi = sem("st_rot_hi")
        st_rot_lo = sem("st_rot_lo")
        st_lat_hi = sem("st_lat_hi")
        st_lat_lo = sem("st_lat_lo")
        kz_turned = sem("kz_turned")
        last_summed = sem("last_summed")
        moments_set = sem("moments_set")
        mean_linked = sem("mean_linked")
        spread_ready = sem("spread_ready")
        x1_set = sem("x1_set")
        x1_turned = sem("x1_turned")
        x1T_set = sem("x1T_set")
        hr_done = sem("hr_done")
        hr_set = sem("hr_set")
        logits_centred = sem("logits_centred")
        logits_exped = sem("logits_exped")
        hw_set = sem("hw_set")
        hw_turned = sem("hw_turned")
        hT_hi_set = sem("hT_hi_set")
        hT_lo_set = sem("hT_lo_set")
        w_hi_set = sem("w_hi_set")
        w_lo_set = sem("w_lo_set")
        x1T_hi_set = sem("x1T_hi_set")
        x1T_lo_set = sem("x1T_lo_set")
        ff_done = sem("ff_done")
        x1b_set = sem("x1b_set")
        ff_added = sem("ff_added")
        ff_stats_set = sem("ff_stats_set")
        rstd_set = sem("rstd_set")
        var_ready = sem("var_ready")
        sd_ready = sem("sd_ready")
        norm_ready = sem("norm_ready")
        res_set = sem("res_set")
        out_written = sem("out_written")

        read_by = {"row": row_maxed, "act": act_read, "dve": dve_read}

        def run_steps(eng, step):
            for g in range(LOOP[0]):
                step(g, g % 2)
            with eng.Fori(LOOP[0], LOOP[1], 2) as g:
                step(g, LOOP[0] % 2)
                step(g + 1, 1 - LOOP[0] % 2)
            for g in range(LOOP[1], PAIRS):
                step(g, g % 2)

        ff_banks = [att_ps[:, 0, :], att_ps[:, 1, :]] + [bank_ps[:, n, :] for n in (0, 1, 2, 3, 4, 5)]
        assert [Use(PAIRS + 1, f"o_{i}").bank for i in range(T)] == [0, 1, 2, 3, 4, 5, 0, 1]

        def parts(g):
            if not isinstance(g, int):
                return True, True, True
            return g + 1 < PAIRS, g >= 1, g >= 2

        block = ctx.enter_context(nc.Block())

        @block.sync
        def _(sp):
            for k in range(KD):
                sp.dma_start(wqd_sb[:, k, :], wq_down[:, k, :]).then_inc(ld_x[k], 16)
                sp.dma_start(xT_sb[:, k, :], xT[:, k, :]).then_inc(ld_x[k], 16)
            sp.dma_start(qw_sb[:, :], qw[0, :, :]).then_inc(ld_qw, 16)
            sp.dma_start(wk_sb, wk).then_inc(ld_k, 16)
            sp.dma_start(cos_sin[:, :, :], tables).then_inc(ld_tab, 16)
            sp.dma_start(id32[:, :], ident).then_inc(ld_id, 16)
            sp.dma_start(id16[:, :], ident16).then_inc(ld_id, 16)
            sp.dma_start(causal16[:, :], mask16).then_inc(ld_id, 16)
            sp.dma_start(ow_sb[:, :], ow[0, :, :]).then_inc(ld_ow, 16)
            for hl, (keys, split) in enumerate(((key_hi, qk_hi_set), (key_lo, qk_lo_set))):
                sp.wait_ge(split, 2)
                for c in range(2):
                    for half in range(2):
                        src, dst = slice(R * half, R * half + R), slice(R * (1 - half), R * (1 - half) + R)
                        cols = slice(c * BANK, (c + 1) * BANK)
                        sp.dma_start(keys[dst, 1 - c, cols].bitcast(F32), keys[src, c, cols].bitcast(F32)).then_inc(keys_swapped, 16)
            sp.dma_start(y[:, :, :], xres.rearrange("(i p) d -> p i d", p=P)).then_inc(ld_y, 16)

            def values_of(*targets):
                return [t if isinstance(t, int) else sp.to_reg(t) for t in targets]

            def maxima(g, h):
                reduced, written, used = values_of(Use(g, f"t{'ab'[h]}_1").read,
                                                   (2 * g + h + 1) * UNF, (2 * g + h - 1) * T)
                sp.wait_ge(dve_read, reduced)
                sp.dma_start(max_dram[h, :].rearrange("(p i) -> p i", i=T), max_col[:, h, :]).then_inc(max_written, 16)
                sp.wait_ge(max_written, written)
                if not isinstance(g, int) or g > 0:
                    sp.wait_ge(centred, used)
                sp.dma_start(maxes[:, h, :], max_dram[h:h + 1, :].partition_broadcast(P).rearrange("p a s -> p (a s)")
                             ).then_inc(max_loaded[h], 16)

            def inverses(g):
                ready0, ready1, written, split = values_of(2 * g - 1, 2 * g, g * (2 * UNF), g - 1)
                sp.wait_ge(inv_ready, ready0)
                sp.dma_start(inv_dram[0, :].rearrange("(p i) -> p i", i=T), inv_col[:, 0, :]).then_inc(inv_written, 16)
                sp.wait_ge(inv_ready, ready1)
                sp.dma_start(inv_dram[1, :].rearrange("(p i) -> p i", i=T), inv_col[:, 1, :]).then_inc(inv_written, 16)
                if not isinstance(g, int) or g > 1:
                    sp.wait_ge(att_lo_set, split)
                sp.wait_ge(inv_written, written)
                for h in range(2):
                    sp.dma_start(att[R * h:R * h + R, :],
                                 inv_dram[h:h + 1, :].partition_broadcast(R).rearrange("p a s -> p (a s)")
                                 ).then_inc(inv_loaded, 16)

            def step(g, par):
                queries, vals, _ = parts(g)
                if queries:
                    sp.wait_ge(st_lat_lo, g + 1)
                    sp.wait_ge(st_rot_hi, 2 * g + 2)
                    sp.wait_ge(st_rot_lo, 2 * g + 2)
                    src = qw[g + 1, :, :] if isinstance(g, int) else qw[bass.ds(g + 1, 1), :, :].rearrange("a p n -> p (a n)")
                    sp.dma_start(qw_sb[:, :], src).then_inc(ld_qw, 16)
                maxima(g, 0)
                maxima(g, 1)
                if vals:
                    inverses(g)
                    sp.wait_ge(n_hi_set, g)
                    src = ow[g, :, :] if isinstance(g, int) else ow[bass.ds(g, 1), :, :].rearrange("a p n -> p (a n)")
                    sp.dma_start(ow_sb[:, :], src).then_inc(ld_ow, 16)

            run_steps(sp, step)
            sp.wait_ge(att_done, PAIRS - 1)
            sp.wait_ge(summed, 2 * T * (PAIRS - 1))
            n = KD * D + KD * HW + D
            for k in range(KD):
                sp.dma_start(base_w[:, k, :], ffn_w[:, k * D:(k + 1) * D]).then_inc(ld_base, 16)
            sp.dma_start(flat[:, KD * D:n], ffn_w[:, KD * D:]).then_inc(ld_ffn, 16)
            sp.dma_start(bias_sb, bias.partition_broadcast(P).rearrange("p a s -> p (a s)")).then_inc(ld_ffn, 16)
            sp.dma_start(flat[:, n + D:n + D + T * NE], rank_tab).then_inc(ld_ffn, 16)
            inverses(PAIRS)
            for i in range(T):
                sp.wait_ge(res_set, i + 1)
                sp.dma_start(out[i * P:(i + 1) * P, :], res[:, i, :]).then_inc(out_written, 16)
            sp.wait_ge(out_written, 16 * T)

        @block.tensor
        def _(pe):
            def open_use(g, name):
                use = Use(g, name)
                for who, count in use.frees():
                    pe.wait_ge(read_by[who], count)
                return use

            def open_job(g, name):
                return bank_ps[:, open_use(g, name).bank, :]

            def queries(g, step_g, chunks):
                if 0 in chunks:
                    pe.wait_ge(st_rot_hi, 2 * g + 2)
                    pe.wait_ge(st_rot_lo, 2 * g + 2)
                    pe.wait_ge(st_lat_hi, 2 * g + 2)
                    pe.wait_ge(st_lat_lo, g + 1)
                    pe.wait_ge(dve_read, Use(step_g, "m").read)
                for c in chunks:
                    s0, s1 = c * BANK, (c + 1) * BANK
                    for name, col in (("z", Z_AT), ("a", A_AT), ("b", B_AT)):
                        o = open_job(step_g, f"f{name}_{c}")
                        w = slice(col, col + P)
                        passes = [(st1_hi[:, w], c1_hi[:, s0:s1]), (st1_hi[:, w], c1_lo[:, s0:s1]),
                                  (st1_lo[:, w], c1_hi[:, s0:s1]), (st2[:, w], c2_hh[:, s0:s1]),
                                  (st2[0:R, w], c2_lo[0:R, s0:s1])]
                        for n, (a, b) in enumerate(passes):
                            mm = pe.matmul(o, a, b, start=(n == 0), stop=(n == len(passes) - 1))
                        mm.then_inc(job_done, 1)

            def fuse_q(g, step_g):
                pe.wait_ge(ld_qw, UNF * (g + 1))
                o = open_job(step_g, "m")
                for n in range(4):
                    half, h = n // 2, n % 2
                    mm = pe.matmul(o[:, n * R:(n + 1) * R], qnT[h][:, half * P:(half + 1) * P], wuk[h],
                                   start=(n == 0), stop=(n == 3), skip_group_check=True)
                mm.then_inc(job_done, 1)

            def score_row(g, h, j):
                bank = open_use(g, f"row{h}{j}").bank
                chunks = 2 if ROW_W[j] > BANK else 1
                w = ROW_W[j] // chunks
                for c in range(chunks):
                    o = bank_ps[:, bank + c, 0:w]
                    q0 = P * j + c * w
                    kk = slice(P * j, P * j + P)
                    pe.matmul(o, key_hi[:, h, kk], q_hi[:, h, q0:q0 + w], start=True, stop=False)
                    pe.matmul(o, key_hi[:, h, kk], q_lo[:, h, q0:q0 + w], start=False, stop=False)
                    if c == 0:
                        pe.matmul(o[:, 0:P], id16[:, :], causal16[:, :], start=False, stop=False)
                    mm = pe.matmul(o, key_lo[:, h, kk], q_hi[:, h, q0:q0 + w], start=False, stop=True)
                mm.then_inc(row_done, 1)

            def turn(g, kind, h, src):
                v = src.rearrange("p (q i) -> p i q", i=T)
                for c in range(2):
                    o = open_job(g, f"{kind}{'ab'[h]}_{c}")
                    for i in range(4):
                        mm = pe.transpose(o[:, P * i:P * i + P], v[:, 4 * c + i, :], id32[:, :])
                    mm.then_inc(job_done, 1)

            def outputs(g, lo, hi):
                if lo == 0:
                    pe.wait_ge(att_hi_set, g - 1)
                    pe.wait_ge(att_lo_set, g - 1)
                    pe.wait_ge(n_hi_set, g - 1)
                    pe.wait_ge(dve_read, Use(g, "n", back=1).read)
                for i in range(lo, hi):
                    if i == T // 2 and isinstance(g, int) and g == PAIRS + 1:
                        pe.wait_ge(att_hi_set, g)
                        pe.wait_ge(att_lo_set, g)
                    o = open_job(g, f"o_{i}")
                    a, b = att_hi[:, i * P:(i + 1) * P], att_lo[:, i * P:(i + 1) * P]
                    pe.matmul(o, a, n_hi[:, :], start=True, stop=False)
                    pe.matmul(o, a, n_lo[:, :], start=False, stop=False)
                    pe.matmul(o, b, n_hi[:, :], start=False, stop=True).then_inc(job_done, 1)

            def fuse_out(g):
                pe.wait_ge(ld_ow, UNF * g)
                o = open_job(g, "n")
                for h in range(2):
                    mm = pe.matmul(o[R * h:R * h + R, :], wuv[h], wout[h], start=True, stop=True)
                mm.then_inc(job_done, 1)

            def attend(g, par, lo, hi):
                if lo == 0 and (not isinstance(g, int) or g > 1):
                    pe.wait_ge(att_scaled, g - 1)
                slot = 2 * (1 - par)
                for j in range(lo, hi):
                    pe.wait_ge(exped, (2 * g - 1) * len(CHUNKS) + CHUNK_OF[j] + 1)
                    for c in range(2):
                        s0, s1 = max(c * BANK, P * j), (c + 1) * BANK
                        if s0 >= s1:
                            continue
                        for h in range(2):
                            mm = pe.matmul(att_ps[R * h:R * h + R, c, s0 - c * BANK:], values[:, j, :],
                                           row(slot + h, j)[:, s0 - P * j:s1 - P * j],
                                           start=(j == 0), stop=(j == 4 * c + 3))
                if hi < T:
                    mm.then_inc(first_half_done, 1)
                else:
                    mm.then_inc(att_done, 1)

            def values_job(step_g, c):
                o = open_job(step_g, f"v_{c}")
                for i in range(4):
                    t = 4 * c + i
                    for k in range(KD):
                        mm = pe.matmul(o[:, i * R:(i + 1) * R], xT_sb[:, k, t * P:(t + 1) * P], wk_sb[:, k, P:P + R],
                                       start=(k == 0), stop=(k == KD - 1))
                mm.then_inc(job_done, 1)

            def turn_maxima(g):
                pe.wait_ge(row_maxed, (2 * g + 1) * T)
                turn(g, "t", 0, top[:, 0, :])
                pe.wait_ge(row_maxed, (2 * g + 2) * T)
                turn(g, "t", 1, top[:, 1, :])

            def step(g, par):
                queries_, vals, output = parts(g)
                pe.wait_ge(qk_hi_set, 4 * g + 6)
                pe.wait_ge(qk_lo_set, 4 * g + 6)
                for h in range(2):
                    for j in range(T):
                        if isinstance(g, int) and g == 0 and (h, j) == (0, 4):
                            pe.wait_ge(keys_swapped, 8 * UNF)
                        score_row(g, h, j)
                if queries_:
                    fuse_q(g + 1, g)
                if vals:
                    pe.wait_ge(summed, (2 * g - 1) * T)
                    turn(g, "l", 0, psum_p[:, 0, :])
                if output and queries_:
                    outputs(g, 0, 4)
                turn_maxima(g)
                if queries_:
                    queries(g + 1, g, (0,))
                if output:
                    outputs(g, 4 if queries_ else 0, 8)
                if queries_:
                    queries(g + 1, g, (1,))
                if isinstance(g, int) and g == 0:
                    values_job(0, 1)
                if vals:
                    fuse_out(g)
                    pe.wait_ge(summed, 2 * g * T)
                    turn(g, "l", 1, psum_p[:, 1, :])
                    attend(g, par, 0, T)

            cq = [open_job(None, f"cq{part + 1}_{c}") for part in range(2) for c in range(2)]
            for k in range(KD):
                pe.wait_ge(ld_x[k], 2 * UNF)
                for n, o in enumerate(cq):
                    part, c = n // 2, n % 2
                    mm = pe.matmul(o, wqd_sb[:, k, part * P:(part + 1) * P], xT_sb[:, k, c * BANK:(c + 1) * BANK],
                                   start=(k == 0), stop=(k == KD - 1))
                    if k == KD - 1:
                        mm.then_inc(job_done, 1)
            fuse_q(0, None)
            pe.wait_ge(ld_k, UNF)
            for c in range(2):
                o = open_job(None, f"k{'ab'[c]}_{c}")
                for k in range(KD):
                    mm = pe.matmul(o, wk_sb[:, k, (c + 1) * P:(c + 2) * P], xT_sb[:, k, c * BANK:(c + 1) * BANK],
                                   start=(k == 0), stop=(k == KD - 1))
                mm.then_inc(job_done, 1)
            o = open_job(None, "kz")
            for k in range(KD):
                for c in range(2):
                    rot = slice(R * (1 - c), R * (1 - c) + R)
                    mm = pe.matmul(o[rot, :], wk_sb[:, k, 0:R], xT_sb[:, k, c * BANK:(c + 1) * BANK],
                                   start=(k == 0), stop=(k == KD - 1))
            mm.then_inc(job_done, 1)
            pe.wait_ge(c_hi_set, 4)
            pe.wait_ge(dve_read, Use(None, "cq2_1").read)
            queries(0, None, (0, 1))
            values_job(None, 0)
            pe.wait_ge(ld_id, 3 * UNF)
            run_steps(pe, step)

            attend(PAIRS, 0, 0, 4)
            pe.wait_ge(summed, (2 * PAIRS - 1) * T)
            turn(PAIRS, "l", 0, psum_p[:, 0, :])
            pe.wait_ge(last_summed, T)
            turn(PAIRS, "l", 1, psum_p[:, 1, :])
            outputs(PAIRS, 0, 8)
            fuse_out(PAIRS)
            attend(PAIRS, 0, 4, T)
            outputs(PAIRS + 1, 0, 8)

            def output_read(i):
                pe.wait_ge(dve_read, Use(PAIRS + 1, f"o_{i}").read)

            def turn_x1(i):
                pe.wait_ge(x1_set, i + 1)
                if i < 2:
                    output_read(2 + i)
                if i >= 2:
                    pe.wait_ge(x1T_set, i - 1)
                for k in range(KD):
                    mm = pe.transpose(bank_ps[:, 2 + i % 2, k * P:(k + 1) * P], y[:, i, k * P:(k + 1) * P], id32[:, :])
                mm.then_inc(x1_turned, 1)

            def down(i):
                pe.wait_ge(x1T_set, i + 1)
                if i < 2:
                    output_read(4 + i)
                if i >= 2:
                    pe.wait_ge(hr_set, i - 1)
                for k in range(KD):
                    mm = pe.matmul(bank_ps[:, 4 + i % 2, 0:HW], x1T[:, k, i * P:(i + 1) * P], hr_w[:, k, :],
                                   start=(k == 0), stop=(k == KD - 1))
                mm.then_inc(hr_done, 1)

            def base(i):
                if i in (2, 3):
                    output_read(4 + i)
                pe.wait_ge(x1T_hi_set, i + 1)
                pe.wait_ge(x1T_lo_set, i + 1)
                for k in range(KD):
                    hi, lo = x1T_hi[i][:, k, :], x1T_lo[i][:, k, :]
                    pe.matmul(ff_banks[i], hi, base_hi[:, k, :], start=(k == 0), stop=False)
                    pe.matmul(ff_banks[i], hi, base_lo[:, k, :], start=False, stop=False)
                    pe.matmul(ff_banks[i], lo, base_hi[:, k, :], start=False, stop=False)

            def lora_up(i):
                pe.wait_ge(hT_lo_set, i // 4 + 1)
                tokens = slice(i * P, (i + 1) * P)
                pe.matmul(ff_banks[i], hT_hi[:, tokens], up_hi, start=False, stop=False)
                pe.matmul(ff_banks[i], hT_hi[:, tokens], up_lo, start=False, stop=False)
                pe.matmul(ff_banks[i], hT_lo[:, tokens], up_hi, start=False, stop=True).then_inc(ff_done, 1)

            pe.wait_ge(ld_ffn, 3 * UNF)
            pe.wait_ge(w_lo_set, 1)
            for i in range(T):
                turn_x1(i)
                if i > 0:
                    down(i - 1)
                if i in (1, 3, 5):
                    base(i // 2)
            down(T - 1)
            pe.wait_ge(x1T_set, T)
            for i in (3, 4, 5):
                base(i)
            pe.wait_ge(hw_set, 1)
            pe.wait_ge(hr_set, T)
            for c in range(2):
                for i in range(4):
                    mm = pe.transpose(bank_ps[:, 4 + c, i * P:(i + 1) * P], hw[:, 4 * c + i, :], id32[:, :])
                mm.then_inc(hw_turned, 1)
            pe.wait_ge(w_lo_set, 2)
            for i in range(6):
                lora_up(i)
            for i in range(6, T):
                base(i)
                lora_up(i)

        @block.scalar
        def _(act):
            def job(g, name):
                use = Use(g, name)
                act.wait_ge(job_done, use.done)
                return bank_ps[:, use.bank, :]

            def rotary_weights(g):
                act.wait_ge(ld_qw, UNF * (g + 1))
                for st, raw in ((st1_hi, wr1), (st2, wr2)):
                    act.activation(rot_cols(st[:, :]), raw.rearrange("p (a b) -> p a b", a=2), ACT.Copy
                                   ).then_inc(st_rot_hi, 1)

            def latent_weights(step_g):
                o = job(step_g, "m")
                for n, st in enumerate((st1_hi, st2)):
                    act.activation(lat_cols(st[:, :]), o[:, n * P:(n + 1) * P].rearrange("p (a b) -> p a b", a=2),
                                   ACT.Copy).then_inc(st_lat_hi, 1)

            def queries(n, step_g):
                for c in range(2):
                    for h in range(2):
                        o = job(step_g, f"f{'ab'[h]}_{c}")
                        lat = slice(R * h, R * h + R)
                        act.wait_ge(qk_lo_set, 4 * n + 2 * c + h + 1)
                        act.wait_ge(rot_set, 4 * n + 2 * c + h + 3)
                        act.activation(fused[lat, h, :], o[lat, :], ACT.Copy).then_inc(act_read, 1)
                    for h in range(2):
                        act.wait_ge(fused_set, 4 * n + 2 * c + h + 3)
                        act.wait_ge(act_read, Use(step_g, f"f{'ab'[h]}_{c}").read)
                        act.activation(q_hi[:, h, c * BANK:(c + 1) * BANK], fused[:, h, :], ACT.Copy
                                       ).then_inc(qk_hi_set, 1)

            def keys():
                for c in range(2):
                    o = job(None, f"k{'ab'[c]}_{c}")
                    lat = slice(R * c, R * c + R)
                    act.wait_ge(rot_set, c + 1)
                    act.activation(fused[lat, c, :], o[lat, :], ACT.Copy).then_inc(act_read, 1)
                for c in range(2):
                    act.wait_ge(fused_set, c + 1)
                    act.wait_ge(act_read, Use(None, f"k{'ab'[c]}_{c}").read)
                    act.activation(key_hi[:, c, c * BANK:(c + 1) * BANK], fused[:, c, :], ACT.Copy
                                   ).then_inc(qk_hi_set, 1)

            def copy_values(step_g, c):
                o = job(step_g, f"v_{c}")
                act.activation(values[:, 4 * c:4 * c + 4, :], o[:, 0:4 * R].rearrange("p (i r) -> p i r", i=4), ACT.Copy
                               ).then_inc(act_read, 1)

            def exp_chunk(head, slot, c):
                js = CHUNKS[c]
                act.wait_ge(centred, head * T + js[-1] + 1)
                part = ring[:, slot, ROW_AT[js[0]]:ROW_AT[js[-1]] + ROW_W[js[-1]]]
                act.activation(part, part, ACT.Exp, scale=SCALE).then_inc(exped, 1)

            def copy_row(g, h, j, slot):
                use = Use(g, f"row{h}{j}")
                act.wait_ge(row_done, use.done)
                w = ROW_W[j]
                if w > BANK:
                    src = bank_ps[:, use.bank:use.bank + 2, 0:w // 2]
                    dst = row(slot, j).rearrange("p (c w) -> p c w", c=2)
                else:
                    src, dst = bank_ps[:, use.bank, 0:w], row(slot, j)
                act.activation(dst, src, ACT.Copy).then_inc(row_copied, 1)

            def split_output(n, cols=slice(0, S)):
                act.wait_ge(att_scaled, n + 1)
                act.activation(att_hi[:, cols], att[:, cols], ACT.Copy).then_inc(att_hi_set, 1)

            def step(g, par):
                queries_, vals, output = parts(g)
                a_slot, old_b = 2 * par, 2 * (1 - par) + 1
                if output:
                    act.wait_ge(att_done, g - 1)
                    act.wait_ge(summed, (2 * g - 2) * T)
                for h in range(2):
                    for j in range(T):
                        copy_row(g, h, j, 2 * par + h)
                        if output and (h, j) == (1, 1):
                            split_output(g - 2)
                        if queries_ and (h, j) == (1, 3):
                            rotary_weights(g + 1)
                        if vals and (h, j) in EXP_B:
                            exp_chunk(2 * g - 1, old_b, EXP_B[h, j])
                if queries_:
                    latent_weights(g)
                    queries(g + 1, g)
                if isinstance(g, int) and g == 0:
                    copy_values(0, 1)
                if vals:
                    act.activation(n_hi[:, :], job(g, "n"), ACT.Copy).then_inc(n_hi_set, 1)
                for c in range(len(CHUNKS)):
                    exp_chunk(2 * g, a_slot, c)

            for part, hi in enumerate((c1_hi, c2_hh)):
                for c in range(2):
                    o = job(None, f"cq{part + 1}_{c}")
                    act.activation(hi[:, c * BANK:(c + 1) * BANK], o, ACT.Copy).then_inc(c_hi_set, 1)
            rotary_weights(0)
            latent_weights(None)
            keys()
            queries(0, None)
            copy_values(None, 0)
            run_steps(act, step)
            for c in range(len(CHUNKS)):
                exp_chunk(2 * PAIRS - 1, 3, c)
            split_output(PAIRS - 2)
            act.wait_ge(ld_base, KD * UNF)
            act.activation(base_hi, base_w, ACT.Copy).then_inc(w_hi_set, 1)
            act.activation(n_hi[:, :], job(PAIRS, "n"), ACT.Copy).then_inc(n_hi_set, 1)
            split_output(PAIRS - 1, slice(0, BANK))
            split_output(PAIRS, slice(BANK, S))

            def copy_x1(i):
                act.wait_ge(x1_turned, i + 1)
                act.activation(x1T[:, :, i * P:(i + 1) * P], bank_ps[:, 2 + i % 2, :].rearrange("p (k s) -> p k s", k=KD),
                               ACT.Copy).then_inc(x1T_set, 1)
                act.wait_ge(x1T_set, i + 1)
                act.activation(x1T_hi[i], x1T[:, :, i * P:(i + 1) * P], ACT.Copy).then_inc(x1T_hi_set, 1)

            for i in range(T):
                act.wait_ge(moments_set, i + 1)
                act.activation(thin[0][:, i:i + 1], moments[:, i, 1:2], ACT.Sqrt, bias=eps_sb).then_inc(spread_ready, 1)
                if i >= 2:
                    copy_x1(i - 2)
            for i in range(T - 2, T):
                copy_x1(i)
            act.wait_ge(ld_ffn, 3 * UNF)
            act.activation(up_hi, up_w, ACT.Copy).then_inc(w_hi_set, 1)
            act.wait_ge(logits_centred, 1)
            act.activation(small[1], small[0], ACT.Exp).then_inc(logits_exped, 1)
            for c in range(2):
                act.wait_ge(hw_turned, c + 1)
                act.activation(hT_hi[:, c * BANK:(c + 1) * BANK], bank_ps[:, 4 + c, :], ACT.Copy
                               ).then_inc(hT_hi_set, 1)

            def apply_norm(i):
                act.wait_ge(norm_ready, i + 1)
                act.activation(res[:, i, :], res[:, i, :], ACT.Identity, scale=thin[9][:, i:i + 1],
                               bias=thin[2][:, i:i + 1]).then_inc(res_set, 1)

            for i in range(T):
                act.wait_ge(var_ready, i + 1)
                act.activation(thin[8][:, i:i + 1], moments[:, i, 1:2], ACT.Sqrt, bias=eps_sb).then_inc(sd_ready, 1)
                if i > 0:
                    apply_norm(i - 1)
            apply_norm(T - 1)

        @block.gpsimd
        def _(pool):
            def rotary_weights(g):
                pool.wait_ge(st_rot_hi, 2 * g + 1)
                if isinstance(g, int) and g == 0:
                    pool.wait_ge(ld_qw, UNF)
                pool.tensor_tensor(rot_cols(st1_lo[:, :]), wr1.rearrange("p (a b) -> p a b", a=2),
                                   rot_cols(st1_hi[:, :].bitcast(F32)), ALU.subtract).then_inc(st_rot_lo, 1)
                pool.wait_ge(st_rot_hi, 2 * g + 2)
                pool.wait_ge(st_rot_lo, 2 * g + 1)
                low = slice(R, P)
                pool.tensor_tensor(rot_cols(st2[low, :]), wr2[low, :].rearrange("p (a b) -> p a b", a=2),
                                   rot_cols(st2[low, :].bitcast(F32)), ALU.subtract).then_inc(st_rot_lo, 1)
                pool.wait_ge(st_rot_lo, 2 * g + 2)

            def queries(n):
                for c in range(2):
                    for h in range(2):
                        if h == 1:
                            pool.wait_ge(fused_set, 4 * n + 2 * c + 3)
                        else:
                            pool.wait_ge(qk_lo_set, 4 * n + 2 * c + 2)
                        pool.wait_ge(rot_set, 4 * n + 2 * c + h + 3)
                        rot = slice(R * (1 - h), R * (1 - h) + R)
                        pool.tensor_tensor(fused[rot, h, :], fused[rot, h, :], turned[rot, :], ALU.add
                                           ).then_inc(fused_set, 1)
                    pool.wait_ge(fused_set, 4 * n + 2 * c + 4)
                    for h in range(2):
                        pool.wait_ge(qk_hi_set, 4 * n + 2 * c + h + 3)
                        cols = slice(c * BANK, (c + 1) * BANK)
                        pool.tensor_tensor(q_lo[:, h, cols], fused[:, h, :], q_hi[:, h, cols].bitcast(F32), ALU.subtract
                                           ).then_inc(qk_lo_set, 1)

            def sum_head(head, h, slot, prev):
                acc = psum_p[:, h, :]
                if prev is not None:
                    pool.wait_ge(job_done, prev)
                for j in range(1, T):
                    pool.wait_ge(exped, head * len(CHUNKS) + CHUNK_OF[j] + 1)
                    if j > 1:
                        pool.wait_ge(summed, head * T + j)
                    before = row(slot, 0)[:, P:] if j == 1 else acc[:, P * j:]
                    pool.tensor_tensor(acc[:, P * j:], before, row(slot, j), ALU.add).then_inc(summed, 1)
                    if j == 1:
                        pool.tensor_copy(acc[:, 0:P], row(slot, 0)[:, 0:P]).then_inc(summed, 1)

            def split_output(n):
                pool.wait_ge(att_hi_set, n + 1)
                pool.tensor_tensor(att_lo[:, :], att[:, :], att_hi[:, :].bitcast(F32), ALU.subtract
                                   ).then_inc(att_lo_set, 1)

            def step(g, par):
                queries_, vals, output = parts(g)
                if output:
                    split_output(g - 2)
                if queries_:
                    rotary_weights(g + 1)
                if vals:
                    sum_head(2 * g - 1, 1, 2 * (1 - par) + 1, Use(g, "lb_1", back=1).done if output else None)
                    pool.wait_ge(summed, 2 * g * T)
                if queries_ and not (isinstance(g, int) and g == 0):
                    queries(g + 1)
                sum_head(2 * g, 0, 2 * par, Use(g, "la_1").done if vals else None)

            rotary_weights(0)
            run_steps(pool, step)
            split_output(PAIRS - 2)

            pool.wait_ge(w_hi_set, 1)
            pool.tensor_tensor(base_lo, base_w, base_hi.bitcast(F32), ALU.subtract).then_inc(w_lo_set, 1)
            for i in range(T):
                pool.wait_ge(x1T_hi_set, i + 1)
                pool.tensor_tensor(x1T_lo[i], x1T[:, :, i * P:(i + 1) * P], x1T_hi[i].bitcast(F32), ALU.subtract
                                   ).then_inc(x1T_lo_set, 1)
            pool.wait_ge(w_hi_set, 2)
            pool.tensor_tensor(up_lo, up_w, up_hi.bitcast(F32), ALU.subtract).then_inc(w_lo_set, 1)
            for i in range(T):
                pool.wait_ge(x1_set, i + 1)
                pool.tensor_tensor(res[:, i, :], y[:, i, :], bias_sb, ALU.add).then_inc(x1b_set, 1)

        @block.vector
        def _(dve):
            def job(g, name):
                use = Use(g, name)
                dve.wait_ge(job_done, use.done)
                return bank_ps[:, use.bank, :]

            def latent_weights(n, step_g):
                o = job(step_g, "m")
                dve.wait_ge(st_lat_hi, 2 * n + 2)
                low = slice(R, P)
                dve.tensor_tensor(lat_cols(st2[low, :]), o[low, P:2 * P].rearrange("p (a b) -> p a b", a=2),
                                  lat_cols(st2[low, :].bitcast(F32)), ALU.subtract).then_inc(st_lat_lo, 1)
                dve.tensor_tensor(lat_cols(st1_lo[:, :]), o[:, 0:P].rearrange("p (a b) -> p a b", a=2),
                                  lat_cols(st1_hi[:, :].bitcast(F32)), ALU.subtract).then_inc(dve_read, 1)

            def rotate(n, step_g, c, between=None):
                cols = slice(c * BANK, (c + 1) * BANK)
                o = job(step_g, f"fz_{c}")
                dve.wait_ge(fused_set, 4 * n + 2 * c + 2)
                dve.tensor_tensor(turned[:, :], o, cos_sin[:, 1, cols], ALU.mult).then_inc(dve_read, 1)
                for h in range(2):
                    if between:
                        between(h)
                    rot = slice(R * (1 - h), R * (1 - h) + R)
                    o = job(step_g, f"f{'ab'[h]}_{c}")
                    dve.wait_ge(qk_lo_set, 4 * n + 2 * c + h + 1)
                    dve.tensor_tensor(fused[rot, h, :], o[rot, :], cos_sin[rot, 0, cols], ALU.mult
                                      ).then_inc(rot_set, 1)

            def split(n, hi, lo, cols, before):
                for h in range(2):
                    rot = slice(R * (1 - h), R * (1 - h) + R)
                    dve.wait_ge(rot_set, before + h + 1)
                    dve.tensor_tensor(fused[rot, h, :], fused[rot, h, :], turned[rot, :], ALU.add
                                      ).then_inc(fused_set, 1)
                for h in range(2):
                    dve.wait_ge(qk_hi_set, before + h + 1)
                    dve.tensor_tensor(lo[:, h, cols[h]], fused[:, h, :], hi[:, h, cols[h]].bitcast(F32), ALU.subtract
                                      ).then_inc(qk_lo_set, 1)

            def queries_alone(n, step_g):
                for c in range(2):
                    rotate(n, step_g, c)
                    split(n, q_hi, q_lo, [slice(c * BANK, (c + 1) * BANK)] * 2, 4 * n + 2 * c + 2)

            def keys():
                for c in range(2):
                    rot = slice(R * (1 - c), R * (1 - c) + R)
                    o = job(None, f"k{'ab'[c]}_{c}")
                    dve.tensor_tensor(fused[rot, c, :], o[rot, :], cos_sin[rot, 0, c * BANK:(c + 1) * BANK], ALU.mult
                                      ).then_inc(rot_set, 1)
                o = job(None, "kz")
                for c in range(2):
                    rot = slice(R * (1 - c), R * (1 - c) + R)
                    ins = dve.tensor_tensor(turned[rot, :], o[rot, :], cos_sin[rot, 1, c * BANK:(c + 1) * BANK], ALU.mult)
                    ins.then_inc(kz_turned if c == 0 else dve_read, 1)
                dve.wait_ge(kz_turned, 1)
                dve.wait_ge(dve_read, Use(None, "kz").read)
                split(0, key_hi, key_lo, [slice(0, BANK), slice(BANK, S)], 0)

            def max_row(g, h, j, slot):
                n = (2 * g + h) * T + j
                use = Use(g, f"row{h}{j}")
                acc = top[:, h, :]
                dve.wait_ge(row_copied, n + 1)
                if j == 0:
                    dve.tensor_copy(acc[:, 0:P], bank_ps[:, use.bank, 0:P]).then_inc(row_maxed, 1)
                    return
                if j > 1:
                    dve.wait_ge(row_maxed, n)
                split = 2 if ROW_W[j] > BANK else 1
                before, after = [t.rearrange("p (c w) -> p c w", c=split) for t in (
                    row(slot, 0)[:, P:] if j == 1 else acc[:, P * j:], acc[:, P * j:])]
                fresh = bank_ps[:, use.bank:use.bank + split, 0:ROW_W[j] // split]
                dve.tensor_tensor(after, before, fresh, ALU.max).then_inc(row_maxed, 1)

            def centre_row(head, h, j, slot):
                if j == 0:
                    dve.wait_ge(max_loaded[h], (head + 2 - h) * (UNF // 2))
                    dve.wait_ge(row_copied, (head + 1) * T)
                r = row(slot, j)
                dve.tensor_tensor(r, r, maxes[:, h, P * j:], ALU.subtract).then_inc(centred, 1)

            def reduce_turned(g, kind, h, col, op):
                for c in range(2):
                    o = job(g, f"{kind}{'ab'[h]}_{c}")
                    dve.tensor_reduce(col[:, h, 4 * c:4 * c + 4], o.rearrange("p (i t) -> p i t", i=4), AX_X, op
                                      ).then_inc(dve_read, 1)

            def invert(g, h):
                dve.wait_ge(dve_read, Use(g, f"l{'ab'[h]}_1").read)
                dve.reciprocal(inv_col[:, h, :], sum_col[:, h, :]).then_inc(inv_ready, 1)

            def add_output(g, lo, hi):
                for i in range(lo, hi):
                    o = job(g, f"o_{i}")
                    dve.tensor_tensor(y[:, i, :], y[:, i, :], o, ALU.add).then_inc(dve_read, 1)

            def scale_latents(n):
                dve.wait_ge(att_done, n + 1)
                dve.wait_ge(inv_loaded, (n + 1) * 2 * UNF)
                dve.tensor_tensor(att[:, :], att[:, :], att_ps[:, :, :].rearrange("p c n -> p (c n)"), ALU.mult
                                  ).then_inc(att_scaled, 1)

            def scale_half(c):
                if c == 0:
                    dve.wait_ge(first_half_done, 1)
                    dve.wait_ge(inv_loaded, PAIRS * 2 * UNF)
                else:
                    dve.wait_ge(att_done, PAIRS)
                cols = slice(c * BANK, (c + 1) * BANK)
                dve.tensor_tensor(att[:, cols], att[:, cols], att_ps[:, c, :], ALU.mult).then_inc(att_scaled, 1)

            def split_half(c):
                cols = slice(c * BANK, (c + 1) * BANK)
                dve.wait_ge(att_hi_set, PAIRS + c)
                dve.tensor_tensor(att_lo[:, cols], att[:, cols], att_hi[:, cols].bitcast(F32), ALU.subtract
                                  ).then_inc(att_lo_set, 1)

            def split_n(g):
                o = job(g, "n")
                dve.wait_ge(n_hi_set, g)
                dve.tensor_tensor(n_lo[:, :], o, n_hi[:, :].bitcast(F32), ALU.subtract).then_inc(dve_read, 1)

            def early_rows(g):
                if isinstance(g, int) and g < 2:
                    return 2 * g
                return T if isinstance(g, int) and g == PAIRS - 1 else EARLY_ROWS

            def step(g, par):
                queries_, vals, output = parts(g)
                a_slot, b_slot, old_b = 2 * par, 2 * par + 1, 2 * (1 - par) + 1
                for j in range(T):
                    max_row(g, 0, j, a_slot)
                    if vals:
                        left = list(range(early_rows(g - 1), T))
                        for k in left[j - 1:j] if 0 < j < T - 1 else left[j - 1:] if j else []:
                            centre_row(2 * g - 1, 1, k, old_b)
                    if output and j == 6:
                        scale_latents(g - 2)
                for j in range(T):
                    max_row(g, 1, j, b_slot)
                if queries_:
                    latent_weights(g + 1, g)
                if vals:
                    reduce_turned(g, "l", 0, sum_col, ALU.add)
                    invert(g, 0)
                if output and queries_:
                    add_output(g, 0, 4)
                reduce_turned(g, "t", 0, max_col, ALU.max)
                reduce_turned(g, "t", 1, max_col, ALU.max)
                centred_rows = 0
                if isinstance(g, int) and g == 0:
                    queries_alone(1, 0)
                elif queries_:
                    rotate(g + 1, g, 0)
                    if output:
                        add_output(g, 4, 8)
                    rotate(g + 1, g, 1, lambda i: centre_row(2 * g, 0, i, a_slot))
                    for j in (2, 3):
                        centre_row(2 * g, 0, j, a_slot)
                    centred_rows = 4
                else:
                    add_output(g, 0, 8)
                if vals:
                    split_n(g)
                    reduce_turned(g, "l", 1, sum_col, ALU.add)
                    invert(g, 1)
                for j in range(centred_rows, T):
                    centre_row(2 * g, 0, j, a_slot)
                for j in range(early_rows(g)):
                    centre_row(2 * g + 1, 1, j, b_slot)
                    if not queries_ and j == 0:
                        scale_latents(g - 1)

            n = 0
            for part, (hi, lo) in enumerate(((c1_hi, c1_lo), (c2_hh, c2_lo))):
                for c in range(2):
                    o = job(None, f"cq{part + 1}_{c}")
                    n += 1
                    dve.wait_ge(c_hi_set, n)
                    rows = slice(0, P if part == 0 else R)
                    cols = slice(c * BANK, (c + 1) * BANK)
                    dve.tensor_tensor(lo[rows, cols], o[rows, :], hi[rows, cols].bitcast(F32), ALU.subtract
                                      ).then_inc(dve_read, 1)
            dve.wait_ge(ld_tab, UNF)
            latent_weights(0, None)
            keys()
            queries_alone(0, None)
            dve.wait_ge(ld_y, UNF)
            run_steps(dve, step)

            acc, slot = psum_p[:, 1, :], 3
            dve.wait_ge(job_done, Use(PAIRS - 1, "lb_1").done)
            for j in range(1, T):
                dve.wait_ge(exped, (2 * PAIRS - 1) * len(CHUNKS) + CHUNK_OF[j] + 1)
                if j > 1:
                    dve.wait_ge(last_summed, j)
                before = row(slot, 0)[:, P:] if j == 1 else acc[:, P * j:]
                dve.tensor_tensor(acc[:, P * j:], before, row(slot, j), ALU.add).then_inc(last_summed, 1)
                if j == 1:
                    dve.tensor_copy(acc[:, 0:P], row(slot, 0)[:, 0:P]).then_inc(last_summed, 1)
            for h in range(2):
                reduce_turned(PAIRS, "l", h, sum_col, ALU.add)
                invert(PAIRS, h)
            add_output(PAIRS, 0, 8)
            scale_half(0)
            split_n(PAIRS)
            split_half(0)
            scale_half(1)
            split_half(1)

            linked = [0]

            def link(ins):
                linked[0] += 1
                ins.then_inc(mean_linked, 1)
                dve.wait_ge(mean_linked, linked[0])

            link(dve.memset(eps_sb, EPS))

            def normalise(i):
                dve.wait_ge(spread_ready, i + 1)
                link(dve.reciprocal(thin[1][:, i:i + 1], thin[0][:, i:i + 1]))
                dve.tensor_scalar(y[:, i, :], y[:, i, :], moments[:, i, 0:1], thin[1][:, i:i + 1], ALU.subtract, ALU.mult
                                  ).then_inc(x1_set, 1)

            def copy_down(i):
                dve.wait_ge(hr_done, i + 1)
                dve.tensor_copy(hr[:, i, :], bank_ps[:, 4 + i % 2, 0:HW]).then_inc(hr_set, 1)

            for i in range(T):
                add_output(PAIRS + 1, i, i + 1)
                dve.wait_ge(dve_read, Use(PAIRS + 1, f"o_{i}").read)
                link(dve.bn_stats(stats[:, i, :], y[:, i, :]))
                dve.bn_aggr(moments[:, i, :], stats[:, i, :]).then_inc(moments_set, 1)
                if i > 0:
                    normalise(i - 1)
                if i > 3:
                    copy_down(i - 4)
            normalise(T - 1)
            for i in range(T - 4, T):
                copy_down(i)
            dve.wait_ge(hr_set, T)

            def over(t):
                return t.unsqueeze(2).broadcast_to([P, T, NE])

            logits = hr[:, :, NE * RANK:]
            centred_l, probs, is_top, ranked, first, rest, second, weight = small
            top1, total, inv_total, at1, top2, at2 = thin[2:8]
            link(dve.tensor_reduce(top1, logits, AX_X, ALU.max))
            dve.tensor_tensor(centred_l, logits, over(top1), ALU.subtract).then_inc(logits_centred, 1)
            dve.wait_ge(logits_exped, 1)
            link(dve.tensor_reduce(total, probs, AX_X, ALU.add))
            link(dve.reciprocal(inv_total, total))
            link(dve.tensor_tensor(probs, probs, over(inv_total), ALU.mult))

            dve.wait_ge(ld_ffn, 3 * UNF)

            def take_largest(values_, largest, place, chosen):
                link(dve.tensor_reduce(largest, values_, AX_X, ALU.max))
                link(dve.tensor_tensor(is_top, values_, over(largest), ALU.is_equal))
                link(dve.tensor_tensor(ranked, is_top, rank_sb, ALU.mult))
                link(dve.tensor_reduce(place, ranked, AX_X, ALU.max))
                link(dve.tensor_tensor(chosen, rank_sb, over(place), ALU.is_equal))

            take_largest(probs, top1, at1, first)
            link(dve.scalar_tensor_tensor(out=rest, in0=first, scalar=-2.0, in1=probs, op0=ALU.mult, op1=ALU.add))
            take_largest(rest, top2, at2, second)
            link(dve.tensor_tensor(weight, first, second, ALU.add))
            link(dve.tensor_tensor(weight, weight, probs, ALU.mult))
            link(dve.tensor_tensor(total, top1, top2, ALU.add))
            link(dve.reciprocal(inv_total, total))
            link(dve.scalar_tensor_tensor(out=weight, in0=weight, scalar=LORA_SCALE, in1=over(inv_total),
                                          op0=ALU.mult, op1=ALU.mult))
            for i in range(T):
                ins = dve.tensor_tensor(hw[:, i, :].rearrange("p (e r) -> p e r", e=NE),
                                        hr[:, i, 0:NE * RANK].rearrange("p (e r) -> p e r", e=NE),
                                        weight[:, i, :].unsqueeze(2).broadcast_to([P, NE, RANK]), ALU.mult)
            ins.then_inc(hw_set, 1)

            for c in range(2):
                cols = slice(c * BANK, (c + 1) * BANK)
                dve.wait_ge(hT_hi_set, c + 1)
                dve.tensor_tensor(hT_lo[:, cols], bank_ps[:, 4 + c, :], hT_hi[:, cols].bitcast(F32), ALU.subtract
                                  ).then_inc(hT_lo_set, 1)

            for i in range(T + 2):
                a, b, c = i, i - 1, i - 2
                if a < T:
                    dve.wait_ge(x1b_set, a + 1)
                    dve.wait_ge(ff_done, a + 1)
                    dve.tensor_tensor(res[:, a, :], res[:, a, :], ff_banks[a], ALU.add).then_inc(ff_added, 1)
                if 0 <= b < T:
                    dve.wait_ge(ff_added, b + 1)
                    dve.bn_stats(stats[:, b, :], res[:, b, :]).then_inc(ff_stats_set, 1)
                if c >= 0:
                    dve.wait_ge(sd_ready, c + 1)
                    dve.reciprocal(thin[9][:, c:c + 1], thin[8][:, c:c + 1]).then_inc(rstd_set, 1)
                if 0 <= b < T:
                    dve.wait_ge(ff_stats_set, b + 1)
                    dve.bn_aggr(moments[:, b, :], stats[:, b, :]).then_inc(var_ready, 1)
                if c >= 0:
                    dve.wait_ge(rstd_set, c + 1)
                    dve.scalar_tensor_tensor(out=thin[2][:, c:c + 1], in0=moments[:, c, 0:1], scalar=-1.0,
                                             in1=thin[9][:, c:c + 1], op0=ALU.mult, op1=ALU.mult
                                             ).then_inc(norm_ready, 1)


def kernel(**inputs):
    import numpy as np
    import concourse.bacc as bacc
    from concourse import mybir as mb
    from concourse.bass_utils import run_bass_kernel_spmd

    def get(name):
        return np.asarray(inputs[name])

    def tiles(a):
        return np.ascontiguousarray(a.reshape(-1, 128, a.shape[-1]).transpose(1, 0, 2))

    def swap(a):
        return np.concatenate([a[..., 32:], a[..., :32]], -1)

    x = get("L0_attn_hidden_states")[0]
    w_qd = get("L0_attn_w_q_down")
    w_kv, w_kr = get("L0_attn_w_kv_down"), get("L0_attn_w_k_rope")
    nope = get("L0_attn_w_q_up_nope").reshape(192, 32, 128).transpose(1, 2, 0)
    nope = np.concatenate([nope, nope[:, :, 128:]], -1)
    nope = nope.reshape(16, 2, 128, 256).transpose(0, 2, 1, 3).reshape(16, 128, 512)
    uk = get("L0_attn_w_uk").reshape(16, 2, 128, 64).transpose(0, 2, 1, 3).reshape(16, 128, 128)
    rope = get("L0_attn_w_q_up_rope").reshape(192, 16, 2, 64).transpose(1, 0, 2, 3)
    rot = np.concatenate([swap(rope[:, :, 1]), swap(rope[:, :, 0]), rope[:, :, 0], rope[:, :, 1]], -1)
    qw = np.concatenate([nope, uk, rot[:, 0:128], np.concatenate([rot[:, 128:], rot[:, 128:]], 1)], -1)
    uv = get("L0_attn_w_uv").reshape(16, 2, 128, 64).transpose(0, 2, 1, 3).reshape(16, 128, 128)
    wo = get("L0_attn_w_out").reshape(16, 2, 128, 512).transpose(0, 2, 1, 3).reshape(16, 128, 1024)

    f32 = np.float32
    freqs = f32(1.0) / f32(10000.0) ** (np.arange(0, 64, 2, dtype=f32) / f32(64))
    ramp = np.clip((f32(2.0 * np.pi) / freqs / f32(4096.0) - f32(1.0)) / f32(31.0), f32(0), f32(1))
    inv_freq = freqs / (f32(1.0) - ramp + ramp * f32(40.0))
    angle = (np.arange(1024, dtype=f32)[:, None] * inv_freq[None, :]).T
    cos, sin = np.cos(angle), np.sin(angle)
    tables = np.stack([np.tile(cos, (4, 1)), np.concatenate([-sin, sin, -sin, sin], 0)], 1).astype(f32)

    import ml_dtypes
    t = np.arange(128)
    arrays = {
        "in_xT": np.ascontiguousarray(tiles(np.ascontiguousarray(x.T))),
        "in_x": x,
        "in_wq_down": tiles(np.concatenate([w_qd, w_qd[:, 128:]], -1)),
        "in_wk": tiles(np.concatenate([swap(w_kr), swap(w_kr), w_kv, w_kr, w_kr, w_kv], -1)),
        "in_qw": qw, "in_ow": np.concatenate([uv, wo], -1),
        "in_tables": tables,
        "in_ident": np.eye(128, dtype=f32),
        "in_ident16": np.eye(128, dtype=f32).astype(ml_dtypes.bfloat16),
        "in_mask16": np.where(t[None, :] < t[:, None], f32(-3e38), f32(0)).astype(ml_dtypes.bfloat16),
        "in_rank": np.tile(np.arange(8, 0, -1).astype(f32), (128, 8)),
        "in_ffn": np.concatenate([
            tiles(get("L0_ffn_W_base").T).reshape(128, -1),
            tiles(np.concatenate([get("L0_ffn_A").reshape(128, 512).T, get("L0_ffn_W_router").T], -1)).reshape(128, -1),
            get("L0_ffn_B").transpose(0, 2, 1).reshape(128, 512)], -1),
        "in_bias": get("L0_ffn_b_base")[None, :],
    }
    arrays = {k: np.ascontiguousarray(v) for k, v in arrays.items()}
    nc = bacc.Bacc("TRN2", target_bir_lowering=False, num_devices=1)
    args = [nc.dram_tensor(k, v.shape, mb.dt.from_np(v.dtype), kind="ExternalInput").ap() for k, v in arrays.items()]
    out = nc.dram_tensor("out", (1024, 512), mb.dt.float32, kind="ExternalOutput").ap()
    build(nc, *args, out)
    r = run_bass_kernel_spmd(nc, [arrays], core_ids=[0])
    return r.results[0]["out"].reshape(1, 1024, 512)
```
